# Optimizing a Trainium2 kernel written in Bass

```python
import numpy as np
import jax
import jax.numpy as jnp

def _softmax(x, axis=-1):
    return jax.nn.softmax(x, axis=axis)

def _gelu(x):
    return jax.nn.gelu(x, approximate=True)

def _silu(x):
    return jax.nn.silu(x)

def _sigmoid(x):
    return jax.nn.sigmoid(x)

def _layernorm(x, axis=-1, eps=1e-05):
    m = jnp.mean(x, axis=axis, keepdims=True)
    v = jnp.var(x, axis=axis, keepdims=True)
    return (x - m) / jnp.sqrt(v + eps)

def _scatter_add(tgt, idx, src, axis=0):
    return tgt.at[idx].add(src)

def _segment_sum(src, seg, n):
    return jax.ops.segment_sum(src, seg, n)
kernel_name = 'mk_adj_resnorm_d2_adj_r2_16d374'

def setup_inputs(seed: int=0):
    np.random.seed(seed)
    _w = jnp.asarray

    def _rec_inputs():
        import jax
        import jax.numpy as jnp
        _gk = jax.random.key(seed)
        x = -9.806e-05 + 1 * jax.random.normal(jax.random.fold_in(_gk, 1), (8192, 64), jnp.float32)
        _w = (1.0 + jnp.arange(8192, dtype=jnp.float32)) ** (-0.5)
        _w = _w / _w.mean()
        _pij = jnp.clip(0.000488281 * _w[:, None] * _w[None, :], 0.0, 1.0)
        _a = jax.random.uniform(jax.random.fold_in(_gk, 2), (8192, 8192)) < _pij
        adj = _a.astype(jnp.int32)
        return (x, adj)
    x, adj = _rec_inputs()

    def _L0_gnn_setup():
        import jax, jax.numpy as jnp
        import numpy as np
        ALPHA = 0.2
        MASK_VAL = -9000000000000000.0
        key = jax.random.key(seed)
        k1, k2, k3 = jax.random.split(key, 3)
        N, D = (4096, 64)
        h = jax.random.normal(k1, (N, D), dtype=jnp.float32)
        adj = jax.random.randint(k2, (N, N), 0, 2, dtype=jnp.int32)
        a = jax.random.normal(k3, (2 * D, 1), dtype=jnp.float32) * (1.414 / np.sqrt(D))
        return {'h': h, 'adj': adj, 'a': a}
    _L0_gnn_all = _L0_gnn_setup()
    _L0_gnn_in = {k: v for k, v in _L0_gnn_all.items() if k in ('a',)}
    del _L0_gnn_all

    def _L1_gnn_setup():
        import jax, jax.numpy as jnp
        import numpy as np
        N = 4096
        F_IN = 64
        F_OUT = 64
        NEG_SLOPE = 0.01
        MASK_FILL = -1000000000000.0
        key = jax.random.key(seed)
        k1, k2, k3, k4 = jax.random.split(key, 4)
        x = jax.random.normal(k1, (N, F_IN), dtype=jnp.float32)
        adj_matrix = jax.random.randint(k2, (N, N), 0, 2, dtype=jnp.int32)
        W = jax.random.normal(k3, (F_IN, F_OUT), dtype=jnp.float32) * (1.0 / np.sqrt(F_IN))
        a = jax.random.normal(k4, (2 * F_IN, 1), dtype=jnp.float32) * (1.0 / np.sqrt(2 * F_IN))
        return {'x': x, 'adj_matrix': adj_matrix, 'W': W, 'a': a}
    _L1_gnn_all = _L1_gnn_setup()
    _L1_gnn_in = {k: v for k, v in _L1_gnn_all.items() if k in ('W', 'a')}
    del _L1_gnn_all
    return {'x': x, 'adj': adj, 'L0_gnn_a': _L0_gnn_in['a'], 'L1_gnn_W': _L1_gnn_in['W'], 'L1_gnn_a': _L1_gnn_in['a']}

def reference(x, adj, L0_gnn_a, L1_gnn_W, L1_gnn_a):
    import jax
    import jax.numpy as jnp

    def _L0_gnn_ref(h, adj, a):
        import jax, jax.numpy as jnp
        import numpy as np
        ALPHA = 0.2
        MASK_VAL = -9000000000000000.0
        D = h.shape[1]
        wh1 = h @ a[:D, :]
        wh2 = h @ a[D:, :]
        e = wh1 + wh2.T
        e = jnp.where(e > 0, e, ALPHA * e)
        scores = jnp.where(adj > 0, e, MASK_VAL)
        attention = jax.nn.softmax(scores, axis=1)
        h_prime = attention @ h
        return jax.nn.relu(h_prime)

    def _L1_gnn_ref(x, adj_matrix, W, a):
        import jax, jax.numpy as jnp
        import numpy as np
        N = 4096
        F_IN = 64
        F_OUT = 64
        NEG_SLOPE = 0.01
        MASK_FILL = -1000000000000.0
        h = x @ W
        a1 = a[:F_OUT, 0]
        a2 = a[F_OUT:, 0]
        f1 = h @ a1
        f2 = h @ a2
        e = jax.nn.leaky_relu(f1[:, None] + f2[None, :], NEG_SLOPE)
        e = jnp.where(adj_matrix > 0, e, MASK_FILL)
        attention = jax.nn.softmax(e, axis=1)
        h_prime = attention @ h
        return jax.nn.elu(h_prime)
    x = _layernorm(x + _L0_gnn_ref(x, adj, L0_gnn_a), axis=-1)
    x = _layernorm(x + _L1_gnn_ref(x, adj, L1_gnn_W, L1_gnn_a), axis=-1)
    return x

_drawn_inputs = setup_inputs


def setup_inputs(seed=0):
    import zlib

    import numpy as np

    out = dict(_drawn_inputs(seed))
    spreads = {}
    factors = {}
    for name, (base, spread) in spreads.items():
        noise = np.random.default_rng([zlib.crc32(name.encode()), seed]).standard_normal(out[name].shape)
        drawn = base * np.exp(spread * noise) if base else spread * noise
        out[name] = jnp.asarray(drawn.astype(out[name].dtype))
    for name, factor in factors.items():
        out[name] = (out[name] * factor).astype(out[name].dtype)
    return out
```

```python
import numpy as np
import concourse.bass as bass
from concourse import mybir
from contextlib import ExitStack

FP32 = mybir.dt.float32
BF16 = mybir.dt.bfloat16
INT32 = mybir.dt.int32
ALU = mybir.AluOpType
ACT = mybir.ActivationFunctionType
AX = mybir.AxisListType

P = 128
N = 8192
F = 64
FE = F + 1
BLOCKS = N // P
GROUPS = 8
GB = BLOCKS // GROUPS
GN = GB * P
JB = 4
BATCHES = BLOCKS // JB
UNROLL = 4
QUADS = BATCHES // UNROLL
PARTS = 3
HALF = GB // 2
BANK = 512
HUGE = 2.0 ** 100
EPS = 1e-5
SLOPES = (0.2, 0.01)
ADJ_SLOTS, RAMP_SLOTS, REST_SLOTS = 4, 4, 2
SLOTS = (RAMP_SLOTS, REST_SLOTS)
LB = GROUPS * BATCHES
LAYER_FREES = 2 + 2 * GROUPS
FREE = 1
PREP_STEPS = 5
FINISH_STEPS = (16, 17)


def cols0(layer):
    return F * layer


def build(nc, x_rows, x_cols, adj_t, a0, a1, w, w_t, out):
    ctx = ExitStack()

    def sb(name, shape, dt=FP32):
        return ctx.enter_context(nc.sbuf_tensor(name, shape, dt))

    def sem(name):
        return ctx.enter_context(nc.semaphore(name))

    with ctx:
        x_sb = sb("x_sb", [P, BLOCKS, F])
        h_sb = sb("h_sb", [P, BLOCKS, FE])
        hs_sb = sb("hs_sb", [P, BLOCKS, 2, PARTS, FE], BF16)
        u_row = sb("u_row", [P, N])
        adj_sb = sb("adj_sb", [P, ADJ_SLOTS, JB, GN], BF16)
        ramp_sb = sb("ramp_sb", [P, RAMP_SLOTS, JB, GN], BF16)
        rest_sb = sb("rest_sb", [P, REST_SLOTS, JB, GN], BF16)
        stage = sb("stage", [P, GB, 2, FE])
        num = sb("num", [P, GB, FE])
        tmp = sb("tmp", [P, GB, FE])
        chunk_sb = tmp[:, :, 0:F]
        xt_sb = stage[0:F, :, :, :].rearrange("p b s f -> p (b s f)")[:, 0:GN]
        ident = sb("ident", [P, P])
        ones = sb("ones", [P, P])
        a_sb = [sb("a0_sb", [F, 2]), sb("a1_sb", [F, 2])]
        w_ext = sb("w_ext", [F, F + 2])
        w_t_sb = sb("w_t_sb", [F, F])
        a_wide = [sb("a0_wide", [F, P]), sb("a1_wide", [F, P])]
        uv = sb("uv", [P, BLOCKS, 2])
        v_huge = sb("v_huge", [P, BLOCKS])
        fac = sb("fac", [P, 4, BLOCKS])
        peak = sb("peak", [P, BLOCKS])
        vmax_part = sb("vmax_part", [P, 1])
        vmax_one = sb("vmax_one", [1, 1])
        vmax = sb("vmax", [P, 1])
        hsum_part = sb("hsum_part", [P, FE])
        hsum = sb("hsum", [P, FE])
        small = sb("small", [P, 6, GB])
        acc = ctx.enter_context(nc.psum_tensor("acc", [P, GB, BANK], FP32))

        consts_loaded = sem("consts_loaded")
        x_loaded = sem("x_loaded")
        xt_loaded = sem("xt_loaded")
        ident_made = sem("ident_made")
        adj_loaded = [sem(f"adj_loaded{i}") for i in range(ADJ_SLOTS)]
        w_projected = sem("w_projected")
        w_ready = sem("w_ready")
        chunk_copied = sem("chunk_copied")
        xt_made = sem("xt_made")
        xt_copied = sem("xt_copied")
        uh_made = sem("uh_made")
        u_copied = sem("u_copied")
        h_copied = sem("h_copied")
        stat_in = sem("stat_in")
        stat_out = sem("stat_out")
        exp_in = sem("exp_in")
        exp_out = sem("exp_out")
        vector_step = sem("vector_step")
        parts_ready = sem("parts_ready")
        ramp_ready = sem("ramp_ready")
        binary_done = sem("binary_done")
        s1_done = sem("s1_done")
        masks_ready = sem("masks_ready")
        masks_used = sem("masks_used")
        half_summed = sem("half_summed")
        first_copied = sem("first_copied")
        acc_free = sem("acc_free")
        mid_added = sem("mid_added")
        stage_read = sem("stage_read")
        elu_in = sem("elu_in")
        elu_out = sem("elu_out")
        norm_in = sem("norm_in")
        norm_ln = sem("norm_ln")
        norm_out = sem("norm_out")
        rows_ready = sem("rows_ready")
        out_sent = sem("out_sent")
        block = ctx.enter_context(nc.Block())

        def of_group(g):
            return bass.ds(g * GB, GB)

        sums = acc[:, :, 0:2 * PARTS * FE].rearrange("p b (s t f) -> p b s t f", s=2, t=PARTS)
        uh = acc[:, 4:6, :].rearrange("p b (k c) -> p b k c", k=GB // 2)

        @block.gpsimd
        def _(pool):
            pool.memset(ident[:, :], 0.0).then_inc(ident_made, 1)
            pool.wait_ge(ident_made, 1)
            pool.affine_select(out=ident[:, :], in_=ident[:, :], compare_op=ALU.not_equal, fill=1.0,
                               base=0, pattern=[[-1, P]], channel_multiplier=1).then_inc(ident_made, 1)

            def load(batch, k):
                pool.dma_start(adj_sb[:, k, :, :].rearrange("p j i -> p (j i)"),
                               adj_t[bass.ds(batch * P, P), :]).then_inc(adj_loaded[k], 16)

            for layer in range(2):
                if layer == 0:
                    for k in range(ADJ_SLOTS):
                        load(k, k)
                with pool.Fori(1 - layer, LB // UNROLL) as q:
                    for k in range(UNROLL):
                        pool.wait_ge(masks_ready, layer * LB + q * UNROLL + k + 1 - ADJ_SLOTS)
                        load(q * UNROLL + k, k)

        @block.sync
        def _(sp):
            for dst, src in ((a_sb[0], a0), (a_sb[1], a1), (w_t_sb, w_t)):
                sp.dma_start(dst[:, :], src).then_inc(consts_loaded, 16)
            sp.dma_start(w_ext[:, 0:F], w).then_inc(consts_loaded, 16)
            sp.dma_start(xt_sb, x_cols[:, 0:GN]).then_inc(xt_loaded, 16)
            sp.dma_start(x_sb[:, :, :], x_rows).then_inc(x_loaded, 16)
            with sp.Fori(1, GROUPS) as c:
                sp.wait_ge(uh_made, c)
                sp.dma_start(xt_sb, x_cols[:, bass.ds(c * GN, GN)]).then_inc(xt_loaded, 16)
            with sp.Fori(0, GROUPS) as g:
                sp.wait_ge(rows_ready, FREE + GROUPS + g + 1)
                sp.dma_start(out[:, of_group(g), :], x_sb[:, of_group(g), :]).then_inc(out_sent, 16)
            sp.wait_ge(out_sent, 16 * GROUPS)

        @block.tensor
        def _(pe):
            pe.sem_inc(masks_used, RAMP_SLOTS)
            pe.sem_inc(xt_made, FREE)
            pe.wait_ge(consts_loaded, 64)
            nc.tensor.matmul(acc[0:F, 0, 0:2], w_t_sb[:, :], a_sb[1][:, :], start=True, stop=True)\
                .then_inc(w_projected, 1)
            pe.wait_ge(w_ready, 1)
            pe.wait_ge(ident_made, 2)

            def prepare(layer):
                cols = 2 if layer == 0 else F + 2
                rhs = a_sb[0] if layer == 0 else w_ext
                if layer == 1:
                    pe.wait_ge(acc_free, LAYER_FREES)
                with pe.Fori(0, GROUPS) as c:
                    if layer == 0:
                        pe.wait_ge(xt_loaded, 16 * c + 16)
                    else:
                        pe.wait_ge(chunk_copied, c + 1)
                        pe.wait_ge(xt_copied, FREE + c)
                        pe.wait_ge(ident_made, 2)
                        for b in range(GB):
                            last = nc.tensor.matmul(acc[0:F, b // 4, (b % 4) * P:(b % 4 + 1) * P],
                                                    chunk_sb[:, b, :], ident[:, :], start=True, stop=True)
                        last.then_inc(xt_made, 1)
                        pe.wait_ge(xt_copied, FREE + c + 1)
                    pe.wait_ge(u_copied, FREE + layer * GROUPS + c)
                    for n in range(GN // BANK):
                        nc.tensor.matmul(acc[:, 2 + n, :], a_wide[layer][:, :],
                                         xt_sb[:, n * BANK:(n + 1) * BANK], start=True, stop=True)
                    for b in range(GB):
                        last = nc.tensor.matmul(uh[:, b // 4, b % 4, 0:cols], xt_sb[:, b * P:(b + 1) * P],
                                                rhs[:, 0:cols], start=True, stop=True)
                    last.then_inc(uh_made, 1)
                pe.wait_ge(stat_in, 2 * layer + 1)
                nc.tensor.transpose(acc[0:1, 6, 0:P], vmax_part[:, :], ident[:, :])
                nc.tensor.matmul(acc[:, 7, 0:FE], ones[:, :], hsum_part[:, :], start=True, stop=True)\
                    .then_inc(stat_out, 1)
                pe.wait_ge(stat_in, 2 * layer + 2)
                nc.tensor.matmul(acc[:, 6, P:P + 1], ones[0:1, :], vmax_one[:, :], start=True, stop=True)\
                    .then_inc(stat_out, 1)

            def quad(layer, g, q, first=False, last=False):
                for k in range(UNROLL):
                    batch = q * UNROLL + k
                    pe.wait_ge(masks_ready, layer * LB + g * BATCHES + batch + 1)
                    for b in range(GB):
                        if first and k == 0 and b % HALF == 0:
                            pe.wait_ge(acc_free, layer * LAYER_FREES + 2 * g + 1 + b // HALF)
                        for j in range(JB):
                            for s, mask in enumerate((ramp_sb, rest_sb)):
                                ins = nc.tensor.matmul(
                                    acc[:, b, s * PARTS * FE:(s + 1) * PARTS * FE],
                                    mask[:, k % SLOTS[s], j, b * P:(b + 1) * P],
                                    hs_sb[:, bass.ds(batch * JB + j, 1), s, :, :].rearrange(
                                        "p o t f -> p (o t f)"),
                                    start=first and k == 0 and j == 0 and s == 0,
                                    stop=last and k == UNROLL - 1 and j == JB - 1 and s == 1,
                                    skip_group_check=True)
                        if last and k == UNROLL - 1 and b == HALF - 1:
                            ins.then_inc(half_summed, 1)
                    ins.then_inc(masks_used, 1)

            for layer in range(2):
                prepare(layer)
                pe.wait_ge(parts_ready, FREE + GROUPS * (layer + 1))
                with pe.Fori(0, GROUPS) as g:
                    quad(layer, g, 0, first=True)
                    with pe.Fori(1, QUADS - 1) as q:
                        quad(layer, g, q)
                    quad(layer, g, QUADS - 1, last=True)

        @block.scalar
        def _(act):
            act.sem_inc(xt_copied, FREE)

            def ramp(layer, g, q, k):
                batch = q * UNROLL + k
                act.wait_ge(masks_used, layer * LB + g * BATCHES + batch + 1)
                first_target = (g + k) * GN - k * GN
                for j in range(JB):
                    ins = nc.scalar.activation(ramp_sb[:, k, j, :], u_row[:, bass.ds(first_target, GN)], ACT.Relu,
                                               bias=v_huge[:, bass.ds(batch * JB + j, 1)], scale=HUGE)
                ins.then_inc(ramp_ready, 1)

            def copy_first(layer, g):
                done = layer * GROUPS + g
                act.wait_ge(stage_read, FREE + done)
                for half in range(2):
                    if half == 0:
                        act.wait_ge(half_summed, done + 1)
                    else:
                        act.wait_ge(masks_used, RAMP_SLOTS + layer * LB + (g + 1) * BATCHES)
                    banks = slice(half * HALF, (half + 1) * HALF)
                    nc.scalar.copy(stage[:, banks, :, :], sums[:, banks, :, 0, :]).then_inc(first_copied, 1)

            def elu_exp(g):
                act.wait_ge(elu_in, g + 1)
                nc.scalar.activation(num[:, :, 0:F], num[:, :, 0:F], ACT.Exp).then_inc(elu_out, 1)

            def norm_root(layer, g):
                done = layer * GROUPS + g
                act.wait_ge(norm_in, done + 1)
                nc.scalar.activation(small[:, 3, :], small[:, 2, :], ACT.Ln).then_inc(norm_ln, 1)
                act.wait_ge(norm_ln, done + 1)
                nc.scalar.activation(small[:, 3, :], small[:, 3, :], ACT.Exp, scale=-0.5).then_inc(norm_out, 1)

            for layer in range(2):
                if layer == 0:
                    act.wait_ge(x_loaded, 16)
                    nc.scalar.copy(h_sb[:, :, 0:F], x_sb[:, :, :]).then_inc(h_copied, 1)
                else:
                    with act.Fori(0, GROUPS) as c:
                        act.wait_ge(xt_made, FREE + c + 1)
                        act.wait_ge(uh_made, GROUPS + c)
                        nc.scalar.copy(xt_sb.rearrange("p (b n) -> p b n", b=2), acc[0:F, 0:2, :])\
                            .then_inc(xt_copied, 1)
                act.wait_ge(exp_in, layer + 1)
                nc.scalar.activation(fac[:, :, :], fac[:, :, :], ACT.Exp).then_inc(exp_out, 1)
                act.wait_ge(u_copied, FREE + (layer + 1) * GROUPS)
                with act.Fori(0, QUADS) as q:
                    for k in range(UNROLL):
                        ramp(layer, 0, q, k)
                with act.Fori(1, GROUPS) as g:
                    ramp(layer, g, 0, 0)
                    ramp(layer, g, 0, 1)
                    copy_first(layer, g - 1)
                    ramp(layer, g, 0, 2)
                    if layer == 1:
                        elu_exp(g - 1)
                    ramp(layer, g, 0, 3)
                    norm_root(layer, g - 1)
                    with act.Fori(1, QUADS) as q:
                        for k in range(UNROLL):
                            ramp(layer, g, q, k)
                copy_first(layer, GROUPS - 1)
                if layer == 1:
                    elu_exp(GROUPS - 1)
                norm_root(layer, GROUPS - 1)

        @block.vector
        def _(dve):
            count = [0]

            def link(ins, base=None):
                count[0] += 1
                ins.then_inc(vector_step, 1)
                dve.wait_ge(vector_step, count[0] if base is None else base + count[0])

            def wide(ap, n, dim=2):
                shape = [P, GB, n]
                return ap.unsqueeze(dim).to_broadcast(shape)

            tt, ts, stt = nc.vector.tensor_tensor, nc.vector.tensor_scalar, nc.vector.scalar_tensor_tensor

            for free in (u_copied, stage_read, parts_ready, rows_ready):
                dve.sem_inc(free, FREE)
            nc.vector.memset(h_sb[:, :, F:FE], 1.0)
            nc.vector.memset(ones[:, :], 1.0)
            dve.wait_ge(consts_loaded, 64)
            nc.vector.tensor_copy(a_wide[0][:, :], a_sb[0][:, 0:1].to_broadcast([F, P]))
            dve.wait_ge(w_projected, 1)
            link(nc.vector.tensor_copy(w_ext[:, F:F + 2], acc[0:F, 0, 0:2]))
            nc.vector.tensor_copy(a_wide[1][:, :], w_ext[:, F:F + 1].to_broadcast([F, P])).then_inc(w_ready, 1)

            def prepare(layer):
                with dve.Fori(0, GROUPS) as c:
                    if layer == 1:
                        dve.wait_ge(xt_made, FREE + c)
                        nc.vector.tensor_copy(chunk_sb, x_sb[:, of_group(c), :]).then_inc(chunk_copied, 1)
                    dve.wait_ge(uh_made, layer * GROUPS + c + 1)
                    nc.vector.tensor_copy(u_row[:, bass.ds(c * GN, GN)].rearrange("p (b n) -> p b n", b=2),
                                          acc[:, 2:4, :])
                    if layer == 1:
                        nc.vector.tensor_copy(h_sb[:, of_group(c), 0:F].rearrange("p (b k) f -> p b k f", b=2),
                                              uh[:, :, :, 0:F])
                    nc.vector.tensor_copy(uv[:, of_group(c), :].rearrange("p (b k) c -> p b k c", b=2),
                                          uh[:, :, :, cols0(layer):cols0(layer) + 2]).then_inc(u_copied, 1)
                dve.wait_ge(u_copied, FREE + (layer + 1) * GROUPS)
                dve.wait_ge(h_copied, 1)
                nc.vector.reduce_max(vmax_part[:, :], uv[:, :, 1], AX.X)
                nc.vector.reduce_sum(hsum_part[:, :], h_sb[:, :, :].rearrange("p b f -> p f b"), AX.X)\
                    .then_inc(stat_in, 1)
                dve.wait_ge(stat_out, 2 * layer + 1)
                nc.vector.tensor_copy(hsum[:, :], acc[:, 7, 0:FE])
                nc.vector.reduce_max(vmax_one[:, :], acc[0:1, 6, 0:P], AX.X).then_inc(stat_in, 1)
                dve.wait_ge(stat_out, 2 * layer + 2)
                nc.vector.tensor_copy(vmax[:, :], acc[:, 6, P:P + 1]).then_inc(acc_free, 2)
                dve.wait_ge(acc_free, layer * LAYER_FREES + 2)
                ts(v_huge[:, :], uv[:, :, 1], HUGE, None, ALU.mult)
                ts(fac[:, 0, :], uv[:, :, 0], vmax[:, :], None, ALU.add)
                ts(fac[:, 1, :], uv[:, :, 0], vmax[:, :], SLOPES[layer], ALU.add, ALU.mult)
                ts(fac[:, 2, :], uv[:, :, 1], vmax[:, :], None, ALU.subtract)
                link(ts(fac[:, 3, :], uv[:, :, 1], vmax[:, :], SLOPES[layer], ALU.subtract, ALU.mult))
                link(tt(peak[:, :], fac[:, 0, :], fac[:, 1, :], ALU.max))
                tt(fac[:, 0, :], fac[:, 0, :], peak[:, :], ALU.subtract)
                tt(fac[:, 1, :], fac[:, 1, :], peak[:, :], ALU.subtract).then_inc(exp_in, 1)
                dve.wait_ge(exp_out, layer + 1)
                start = count[0]
                with dve.Fori(0, GROUPS) as c:
                    base = c * PREP_STEPS
                    blocks = of_group(c)
                    dve.wait_ge(parts_ready, FREE + layer * GROUPS + c)
                    tt(stage[:, :, 0, :], h_sb[:, blocks, :], wide(fac[:, 2, blocks], FE), ALU.mult)
                    link(tt(stage[:, :, 1, :], h_sb[:, blocks, :], wide(fac[:, 3, blocks], FE), ALU.mult), base)
                    for part in range(PARTS):
                        dst = hs_sb[:, blocks, :, part, :]
                        if part < PARTS - 1:
                            link(nc.vector.tensor_copy(dst, stage[:, :, :, :]), base)
                            link(tt(stage[:, :, :, :], stage[:, :, :, :], dst, ALU.subtract), base)
                        else:
                            nc.vector.tensor_copy(dst, stage[:, :, :, :]).then_inc(parts_ready, 1)
                assert count[0] - start == PREP_STEPS
                count[0] += (GROUPS - 1) * PREP_STEPS

            def masks(layer, g, q, k):
                t = layer * LB + g * BATCHES + q * UNROLL + k
                adj, s1, s2 = adj_sb[:, k, :, :], ramp_sb[:, k, :, :], rest_sb[:, k % REST_SLOTS, :, :]
                dve.wait_ge(adj_loaded[k], 16 * (layer * LB // UNROLL + g * QUADS + q + 1))
                ts(adj, adj, 0.0, None, ALU.is_gt).then_inc(binary_done, 1)
                dve.wait_ge(binary_done, t + 1)
                dve.wait_ge(ramp_ready, t + 1)
                tt(s1, s1, adj, ALU.min).then_inc(s1_done, 1)
                dve.wait_ge(s1_done, t + 1)
                dve.wait_ge(masks_used, t + 1 + RAMP_SLOTS - REST_SLOTS)
                tt(s2, adj, s1, ALU.subtract).then_inc(masks_ready, 1)

            def add_parts(layer, g):
                for half in range(2):
                    banks = slice(half * HALF, (half + 1) * HALF)
                    dve.wait_ge(first_copied, 2 * (layer * GROUPS + g) + half + 1)
                    step = layer * GROUPS * 2 + 2 * g + half
                    tt(stage[:, banks, :, :], stage[:, banks, :, :], sums[:, banks, :, 1, :], ALU.add)\
                        .then_inc(mid_added, 1)
                    dve.wait_ge(mid_added, step + 1)
                    tt(stage[:, banks, :, :], stage[:, banks, :, :], sums[:, banks, :, 2, :], ALU.add)\
                        .then_inc(acc_free, 1)

            def attend(layer, g, base):
                rows = of_group(g)
                dve.wait_ge(acc_free, layer * LAYER_FREES + 2 + 2 * (g + 1))
                dve.wait_ge(rows_ready, FREE + layer * GROUPS + g)
                tt(num[:, :, :], stage[:, :, 0, :], wide(fac[:, 0, rows], FE), ALU.mult)
                link(tt(tmp[:, :, :], stage[:, :, 1, :], wide(fac[:, 1, rows], FE), ALU.mult), base)
                tt(num[:, :, :], num[:, :, :], tmp[:, :, :], ALU.add).then_inc(stage_read, 1)
                dve.wait_ge(stage_read, FREE + layer * GROUPS + g + 1)
                link(ts(small[:, 0, :], num[:, :, F], 0.0, None, ALU.is_equal), base)
                link(tt(tmp[:, :, :], wide(hsum[:, :], FE, 1), wide(small[:, 0, :], FE), ALU.mult), base)
                link(tt(num[:, :, :], num[:, :, :], tmp[:, :, :], ALU.add), base)
                link(nc.vector.reciprocal(small[:, 1, :], num[:, :, F]), base)
                link(tt(tmp[:, :, 0:F], num[:, :, 0:F], wide(small[:, 1, :], F), ALU.mult), base)
                y, o = num[:, :, 0:F], tmp[:, :, 0:F]
                if layer == 0:
                    link(stt(y, o, 0.0, x_sb[:, rows, :], ALU.max, ALU.add), base)
                else:
                    ts(y, o, 0.0, None, ALU.min).then_inc(elu_in, 1)

            def residual(layer, g, base):
                rows = of_group(g)
                y, o = num[:, :, 0:F], tmp[:, :, 0:F]
                if layer == 1:
                    dve.wait_ge(elu_out, g + 1)
                    link(stt(y, o, 0.0, y, ALU.max, ALU.add), base)
                    link(stt(y, y, -1.0, x_sb[:, rows, :], ALU.add, ALU.add), base)
                link(nc.vector.reduce_sum(small[:, 0, :], y, AX.X), base)
                link(ts(small[:, 1, :], small[:, 0, :], 1.0 / F, None, ALU.mult), base)
                link(tt(y, y, wide(small[:, 1, :], F), ALU.subtract), base)
                link(tt(o, y, y, ALU.mult), base)
                link(nc.vector.reduce_sum(small[:, 0, :], o, AX.X), base)
                ts(small[:, 2, :], small[:, 0, :], 1.0 / F, EPS, ALU.mult, ALU.add).then_inc(norm_in, 1)

            def normalise(layer, g, base):
                root, t = small[:, 3, :], small[:, 4, :]
                dve.wait_ge(norm_out, layer * GROUPS + g + 1)
                link(tt(t, root, root, ALU.mult), base)
                link(tt(t, t, small[:, 2, :], ALU.mult), base)
                link(ts(t, t, -0.5, 1.5, ALU.mult, ALU.add), base)
                link(tt(small[:, 5, :], root, t, ALU.mult), base)
                tt(x_sb[:, of_group(g), :], num[:, :, 0:F], wide(small[:, 5, :], F), ALU.mult)\
                    .then_inc(rows_ready, 1)

            for layer in range(2):
                if layer == 1:
                    dve.wait_ge(rows_ready, FREE + GROUPS)
                    dve.wait_ge(masks_used, RAMP_SLOTS + LB)
                    dve.wait_ge(ramp_ready, LB)
                prepare(layer)
                with dve.Fori(0, QUADS) as q:
                    for k in range(UNROLL):
                        masks(layer, 0, q, k)
                start, steps = count[0], FINISH_STEPS[layer]
                with dve.Fori(1, GROUPS) as g:
                    base = (g - 1) * steps
                    masks(layer, g, 0, 0)
                    add_parts(layer, g - 1)
                    masks(layer, g, 0, 1)
                    attend(layer, g - 1, base)
                    masks(layer, g, 0, 2)
                    residual(layer, g - 1, base)
                    masks(layer, g, 0, 3)
                    normalise(layer, g - 1, base)
                    with dve.Fori(1, QUADS) as q:
                        for k in range(UNROLL):
                            masks(layer, g, q, k)
                assert count[0] - start == steps
                count[0] = start + (GROUPS - 1) * steps
                add_parts(layer, GROUPS - 1)
                attend(layer, GROUPS - 1, 0)
                residual(layer, GROUPS - 1, 0)
                normalise(layer, GROUPS - 1, 0)
    return nc


def kernel(x, adj, L0_gnn_a, L1_gnn_W, L1_gnn_a):
    import concourse.bacc as bacc
    from concourse.bass_utils import run_bass_kernel_spmd

    x, adj, a0, w, a1 = (np.asarray(v) for v in (x, adj, L0_gnn_a, L1_gnn_W, L1_gnn_a))
    adj_t = adj.reshape(GROUPS, GN, BATCHES, JB, P).transpose(0, 2, 4, 3, 1)
    arrays = {
        "x_rows": x.reshape(BLOCKS, P, F).transpose(1, 0, 2),
        "x_cols": x.T,
        "adj_t": adj_t.reshape(GROUPS * BATCHES * P, JB * GN),
        "a0": a0.reshape(2, F).T,
        "a1": a1.reshape(2, F).T,
        "w": w,
        "w_t": w.T,
    }
    arrays = {name: np.ascontiguousarray(v) for name, v in arrays.items()}
    nc = bacc.Bacc("TRN2", target_bir_lowering=False, num_devices=1)
    args = [nc.dram_tensor(name, v.shape, mybir.dt.from_np(v.dtype), kind="ExternalInput").ap()
            for name, v in arrays.items()]
    out = nc.dram_tensor("out", (P, BLOCKS, F), FP32, kind="ExternalOutput").ap()
    build(nc, *args, out)
    result = run_bass_kernel_spmd(nc, [arrays], core_ids=[0]).results[0]["out"]
    return result.transpose(1, 0, 2).reshape(N, F)
```

```python
import numpy as np
import concourse.bass as bass
from concourse import mybir
from contextlib import ExitStack

FP32 = mybir.dt.float32
BF16 = mybir.dt.bfloat16
FP16 = mybir.dt.float16
INT16 = mybir.dt.int16
UINT16 = mybir.dt.uint16
INT32 = mybir.dt.int32
ALU = mybir.AluOpType
ACT = mybir.ActivationFunctionType
AX = mybir.AxisListType

P = 128
N = 8192
F = 64
FE = F + 1
BLOCKS = N // P
GROUPS = 8
GB = BLOCKS // GROUPS
GN = GB * P
JB = 4
BATCHES = BLOCKS // JB
UNROLL = 4
QUADS = BATCHES // UNROLL
PARTS_PER_QUAD = GROUPS // QUADS
PARTS = 3
HALF = GB // 2
BANK = 512
HUGE = 2.0 ** 100
PLUS_BITS = 0x3C00
EPS = 1e-5
SLOPES = (0.2, 0.01)
ADJ_SLOTS, S1_SLOTS, S2_SLOTS = 4, 2, 4
SLOTS = (S1_SLOTS, S2_SLOTS)
LB = GROUPS * BATCHES
LAYER_FREES = 2 + 2 * GROUPS
FREE = 1
FINISH_STEPS = (16, 17)


def cols0(layer):
    return F * layer


def build(nc, x_rows, x_cols, adj_t, a0, a1, w, w_t, out):
    ctx = ExitStack()

    def sb(name, shape, dt=FP32):
        return ctx.enter_context(nc.sbuf_tensor(name, shape, dt))

    def sem(name):
        return ctx.enter_context(nc.semaphore(name))

    with ctx:
        x_sb = sb("x_sb", [P, BLOCKS, F])
        h_sb = sb("h_sb", [P, BLOCKS, FE])
        hs_sb = sb("hs_sb", [P, BLOCKS, 2, PARTS, FE], BF16)
        u_row = sb("u_row", [P, N])
        adj_sb = sb("adj_sb", [P, ADJ_SLOTS, JB, GN], BF16)
        sign_sb = sb("sign_sb", [P, S2_SLOTS, JB, GN], FP16)
        s1_sb = sb("s1_sb", [P, S1_SLOTS, JB, GN], BF16)
        s2_sb = sign_sb[:, :, :, :].bitcast(BF16)
        stage = sb("stage", [P, GB, 2, FE])
        stage_2 = sb("stage_2", [P, GB, 2, FE])
        num = stage_2[:, :, 0, :]
        tmp = stage_2[:, :, 1, :]
        s1_words = s1_sb[:, :, :, :].rearrange("p k j i -> p k (j i)").bitcast(FP32)
        xt_sb = [s1_words[0:F, k, 0:GN] for k in range(2)]
        chunk_sb = [s1_words[:, k, GN:GN + GB * F].rearrange("p (b f) -> p b f", b=GB) for k in range(2)]
        ident = sb("ident", [P, P])
        ones = sb("ones", [P, P])
        a_sb = [sb("a0_sb", [F, 2]), sb("a1_sb", [F, 2])]
        w_ext = sb("w_ext", [F, F + 2])
        w_t_sb = sb("w_t_sb", [F, F])
        a_wide = [sb("a0_wide", [F, P]), sb("a1_wide", [F, P])]
        uv = sb("uv", [P, BLOCKS, 2])
        v_huge = sb("v_huge", [P, BLOCKS])
        fac = sb("fac", [P, 4, BLOCKS])
        peak = sb("peak", [P, BLOCKS])
        vmax_part = sb("vmax_part", [P, 1])
        vmax_one = sb("vmax_one", [1, 1])
        vmax = sb("vmax", [P, 1])
        hsum_part = sb("hsum_part", [P, FE])
        hsum = sb("hsum", [P, FE])
        small = sb("small", [P, 6, GB])
        acc = ctx.enter_context(nc.psum_tensor("acc", [P, GB, BANK], FP32))

        consts_loaded = sem("consts_loaded")
        x_loaded = sem("x_loaded")
        xt_loaded = [sem(f"xt_loaded{i}") for i in range(2)]
        ident_made = sem("ident_made")
        adj_loaded = [sem(f"adj_loaded{i}") for i in range(ADJ_SLOTS)]
        w_projected = sem("w_projected")
        w_ready = sem("w_ready")
        chunk_copied = sem("chunk_copied")
        xt_made = sem("xt_made")
        xt_copied = sem("xt_copied")
        uh_made = sem("uh_made")
        u_copied = sem("u_copied")
        h_copied = sem("h_copied")
        stat_in = sem("stat_in")
        stat_out = sem("stat_out")
        exp_in = sem("exp_in")
        exp_out = sem("exp_out")
        vector_step = sem("vector_step")
        parts_ready = sem("parts_ready")
        stage_filled = sem("stage_filled")
        part_made = sem("part_made")
        sign_ready = sem("sign_ready")
        adj_read = sem("adj_read")
        masks_ready = sem("masks_ready")
        masks_used = sem("masks_used")
        half_summed = sem("half_summed")
        first_copied = sem("first_copied")
        acc_free = sem("acc_free")
        mid_added = sem("mid_added")
        stage_read = sem("stage_read")
        elu_in = sem("elu_in")
        elu_out = sem("elu_out")
        norm_in = sem("norm_in")
        norm_ln = sem("norm_ln")
        norm_out = sem("norm_out")
        rows_ready = sem("rows_ready")
        out_sent = sem("out_sent")
        block = ctx.enter_context(nc.Block())

        def of_group(g):
            return bass.ds(g * GB, GB)

        sums = acc[:, :, 0:2 * PARTS * FE].rearrange("p b (s t f) -> p b s t f", s=2, t=PARTS)
        t_banks = (acc[0:F, 0:2, :], acc[0:F, 2:4, :])
        u_banks = (acc[:, 4:6, :], acc[:, 0:2, :])
        uh_banks = tuple(b.rearrange("p b (k c) -> p b k c", k=GB // 2) for b in (acc[:, 6:8, :], acc[:, 2:4, :]))

        @block.gpsimd
        def _(pool):
            pool.memset(ident[:, :], 0.0).then_inc(ident_made, 1)
            pool.wait_ge(ident_made, 1)
            pool.affine_select(out=ident[:, :], in_=ident[:, :], compare_op=ALU.not_equal, fill=1.0,
                               base=0, pattern=[[-1, P]], channel_multiplier=1).then_inc(ident_made, 1)

            def load(batch, k):
                pool.dma_start(adj_sb[:, k, :, :].rearrange("p j i -> p (j i)"),
                               adj_t[bass.ds(batch * P, P), :]).then_inc(adj_loaded[k], 16)

            for layer in range(2):
                if layer == 0:
                    for k in range(ADJ_SLOTS):
                        load(k, k)
                with pool.Fori(1 - layer, LB // UNROLL) as q:
                    for k in range(UNROLL):
                        pool.wait_ge(adj_read, layer * LB + q * UNROLL + k + 1 - ADJ_SLOTS)
                        load(q * UNROLL + k, k)

        @block.sync
        def _(sp):
            for dst, src in ((a_sb[0], a0), (a_sb[1], a1), (w_t_sb, w_t)):
                sp.dma_start(dst[:, :], src).then_inc(consts_loaded, 16)
            sp.dma_start(w_ext[:, 0:F], w).then_inc(consts_loaded, 16)
            for k in range(2):
                sp.dma_start(xt_sb[k], x_cols[:, k * GN:(k + 1) * GN]).then_inc(xt_loaded[k], 16)
            sp.dma_start(x_sb[:, :, :], x_rows).then_inc(x_loaded, 16)
            with sp.Fori(1, GROUPS // 2) as i:
                for k in range(2):
                    sp.wait_ge(uh_made, 2 * i + k - 1)
                    sp.dma_start(xt_sb[k], x_cols[:, bass.ds((2 * i + k) * GN, GN)]).then_inc(xt_loaded[k], 16)
            with sp.Fori(0, GROUPS) as g:
                sp.wait_ge(rows_ready, FREE + GROUPS + g + 1)
                sp.dma_start(out[:, of_group(g), :], x_sb[:, of_group(g), :]).then_inc(out_sent, 16)
            sp.wait_ge(out_sent, 16 * GROUPS)

        @block.tensor
        def _(pe):
            pe.sem_inc(masks_used, S2_SLOTS)
            pe.sem_inc(xt_made, FREE)
            pe.wait_ge(consts_loaded, 64)
            nc.tensor.matmul(acc[0:F, 0, 0:2], w_t_sb[:, :], a_sb[1][:, :], start=True, stop=True)\
                .then_inc(w_projected, 1)
            pe.wait_ge(w_ready, 1)
            pe.wait_ge(ident_made, 2)

            def prepare(layer):
                cols = 2 if layer == 0 else F + 2
                rhs = a_sb[0] if layer == 0 else w_ext
                if layer == 1:
                    pe.wait_ge(acc_free, LAYER_FREES)
                with pe.Fori(0, GROUPS // 2) as i:
                    if layer == 1:
                        for k in range(2):
                            pe.wait_ge(chunk_copied, 2 * i + k + 1)
                            pe.wait_ge(u_copied, FREE + GROUPS + 2 * i)
                            for b in range(GB):
                                columns = slice((b % 4) * P, (b % 4 + 1) * P)
                                last = nc.tensor.matmul(t_banks[k][:, b // 4, columns], chunk_sb[k][:, b, :],
                                                        ident[:, :], start=True, stop=True)
                            last.then_inc(xt_made, 1)
                    for k in range(2):
                        if layer == 0:
                            pe.wait_ge(xt_loaded[k], 16 * i + 16)
                            pe.wait_ge(u_copied, FREE + 2 * i)
                        else:
                            pe.wait_ge(xt_copied, FREE + 2 * i + k + 1)
                        for n in range(GN // BANK):
                            nc.tensor.matmul(u_banks[k][:, n, :], a_wide[layer][:, :],
                                             xt_sb[k][:, n * BANK:(n + 1) * BANK], start=True, stop=True)
                        for b in range(GB):
                            last = nc.tensor.matmul(uh_banks[k][:, b // 4, b % 4, 0:cols],
                                                    xt_sb[k][:, b * P:(b + 1) * P], rhs[:, 0:cols],
                                                    start=True, stop=True)
                        last.then_inc(uh_made, 1)
                pe.wait_ge(stat_in, 2 * layer + 1)
                nc.tensor.transpose(acc[0:1, 6, 0:P], vmax_part[:, :], ident[:, :])
                nc.tensor.matmul(acc[:, 7, 0:FE], ones[:, :], hsum_part[:, :], start=True, stop=True)\
                    .then_inc(stat_out, 1)
                pe.wait_ge(stat_in, 2 * layer + 2)
                nc.tensor.matmul(acc[:, 6, P:P + 1], ones[0:1, :], vmax_one[:, :], start=True, stop=True)\
                    .then_inc(stat_out, 1)

            def quad(layer, g, q, first=False, last=False):
                if not first:
                    pe.wait_ge(parts_ready, FREE + layer * GROUPS + PARTS_PER_QUAD * (q + 1))
                for k in range(UNROLL):
                    batch = q * UNROLL + k
                    pe.wait_ge(masks_ready, layer * LB + g * BATCHES + batch + 1)
                    for b in range(GB):
                        if first and k == 0 and b % HALF == 0:
                            pe.wait_ge(acc_free, layer * LAYER_FREES + 2 * g + 1 + b // HALF)
                        for j in range(JB):
                            for s, mask in enumerate((s1_sb, s2_sb)):
                                ins = nc.tensor.matmul(
                                    acc[:, b, s * PARTS * FE:(s + 1) * PARTS * FE],
                                    mask[:, k % SLOTS[s], j, b * P:(b + 1) * P],
                                    hs_sb[:, bass.ds(batch * JB + j, 1), s, :, :].rearrange(
                                        "p o t f -> p (o t f)"),
                                    start=first and k == 0 and j == 0 and s == 0,
                                    stop=last and k == UNROLL - 1 and j == JB - 1 and s == 1,
                                    skip_group_check=True)
                        if last and k == UNROLL - 1 and b == HALF - 1:
                            ins.then_inc(half_summed, 1)
                    ins.then_inc(masks_used, 1)

            for layer in range(2):
                prepare(layer)
                pe.wait_ge(parts_ready, FREE + layer * GROUPS + PARTS_PER_QUAD)
                with pe.Fori(0, GROUPS) as g:
                    quad(layer, g, 0, first=True)
                    with pe.Fori(1, QUADS - 1) as q:
                        quad(layer, g, q)
                    quad(layer, g, QUADS - 1, last=True)

        @block.scalar
        def _(act):
            act.sem_inc(xt_copied, FREE)

            def sign(layer, g, q, k):
                batch = q * UNROLL + k
                act.wait_ge(masks_used, layer * LB + g * BATCHES + batch + 1)
                first_target = (g + k) * GN - k * GN
                for j in range(JB):
                    ins = nc.scalar.activation(sign_sb[:, k, j, :], u_row[:, bass.ds(first_target, GN)], ACT.Sign,
                                               bias=v_huge[:, bass.ds(batch * JB + j, 1)])
                ins.then_inc(sign_ready, 1)

            def round_parts(layer, pair):
                for part in range(PARTS):
                    for k, buffer in enumerate((stage, stage_2)):
                        act.wait_ge(stage_filled, 2 * PARTS * (layer * GROUPS // 2 + pair) + 2 * part + k + 1)
                        ins = nc.scalar.copy(hs_sb[:, of_group(2 * pair + k), :, part, :], buffer[:, :, :, :])
                        ins.then_inc(part_made if part < PARTS - 1 else parts_ready, 1)

            def copy_first(layer, g):
                done = layer * GROUPS + g
                act.wait_ge(stage_read, FREE + done)
                for half in range(2):
                    if half == 0:
                        act.wait_ge(half_summed, done + 1)
                    else:
                        act.wait_ge(masks_used, S2_SLOTS + layer * LB + (g + 1) * BATCHES)
                    banks = slice(half * HALF, (half + 1) * HALF)
                    nc.scalar.copy(stage[:, banks, :, :], sums[:, banks, :, 0, :]).then_inc(first_copied, 1)

            def elu_exp(g):
                act.wait_ge(elu_in, g + 1)
                nc.scalar.activation(num[:, :, 0:F], num[:, :, 0:F], ACT.Exp).then_inc(elu_out, 1)

            def norm_root(layer, g):
                done = layer * GROUPS + g
                act.wait_ge(norm_in, done + 1)
                nc.scalar.activation(small[:, 3, :], small[:, 2, :], ACT.Ln).then_inc(norm_ln, 1)
                act.wait_ge(norm_ln, done + 1)
                nc.scalar.activation(small[:, 3, :], small[:, 3, :], ACT.Exp, scale=-0.5).then_inc(norm_out, 1)

            for layer in range(2):
                if layer == 0:
                    act.wait_ge(x_loaded, 16)
                    nc.scalar.copy(h_sb[:, :, 0:F], x_sb[:, :, :]).then_inc(h_copied, 1)
                else:
                    with act.Fori(0, GROUPS // 2) as i:
                        for k in range(2):
                            act.wait_ge(xt_made, FREE + 2 * i + k + 1)
                            nc.scalar.copy(xt_sb[k].rearrange("p (b n) -> p b n", b=2), t_banks[k])\
                                .then_inc(xt_copied, 1)
                act.wait_ge(exp_in, layer + 1)
                nc.scalar.activation(fac[:, :, :], fac[:, :, :], ACT.Exp).then_inc(exp_out, 1)
                act.wait_ge(u_copied, FREE + (layer + 1) * GROUPS)
                round_parts(layer, 0)
                for q in range(QUADS):
                    sign(layer, 0, q, 0)
                    sign(layer, 0, q, 1)
                    if q < QUADS - 1:
                        round_parts(layer, q + 1)
                    sign(layer, 0, q, 2)
                    sign(layer, 0, q, 3)
                with act.Fori(1, GROUPS) as g:
                    sign(layer, g, 0, 0)
                    sign(layer, g, 0, 1)
                    copy_first(layer, g - 1)
                    sign(layer, g, 0, 2)
                    if layer == 1:
                        elu_exp(g - 1)
                    sign(layer, g, 0, 3)
                    norm_root(layer, g - 1)
                    with act.Fori(1, QUADS) as q:
                        for k in range(UNROLL):
                            sign(layer, g, q, k)
                copy_first(layer, GROUPS - 1)
                if layer == 1:
                    elu_exp(GROUPS - 1)
                norm_root(layer, GROUPS - 1)

        @block.vector
        def _(dve):
            count = [0]

            def link(ins, base=None):
                count[0] += 1
                ins.then_inc(vector_step, 1)
                dve.wait_ge(vector_step, count[0] if base is None else base + count[0])

            def wide(ap, n, dim=2):
                shape = [P, GB, n]
                return ap.unsqueeze(dim).to_broadcast(shape)

            tt, ts, stt = nc.vector.tensor_tensor, nc.vector.tensor_scalar, nc.vector.scalar_tensor_tensor

            for free in (u_copied, stage_read, parts_ready, rows_ready):
                dve.sem_inc(free, FREE)
            nc.vector.memset(h_sb[:, :, F:FE], 1.0)
            nc.vector.memset(ones[:, :], 1.0)
            dve.wait_ge(consts_loaded, 64)
            ts(a_wide[0][:, :], a_sb[0][:, 0:1].to_broadcast([F, P]), HUGE, None, ALU.mult)
            dve.wait_ge(w_projected, 1)
            link(nc.vector.tensor_copy(w_ext[:, F:F + 2], acc[0:F, 0, 0:2]))
            ts(a_wide[1][:, :], w_ext[:, F:F + 1].to_broadcast([F, P]), HUGE, None, ALU.mult).then_inc(w_ready, 1)

            def prepare(layer):
                with dve.Fori(0, GROUPS // 2) as i:
                    if layer == 1:
                        for k in range(2):
                            dve.wait_ge(xt_made, FREE + 2 * i + k)
                            nc.vector.tensor_copy(chunk_sb[k], x_sb[:, of_group(2 * i + k), :])\
                                .then_inc(chunk_copied, 1)
                    for k in range(2):
                        c = 2 * i + k
                        dve.wait_ge(uh_made, layer * GROUPS + c + 1)
                        ts(u_row[:, bass.ds(c * GN, GN)].bitcast(INT32).rearrange("p (b n) -> p b n", b=2),
                           u_banks[k].bitcast(INT32), -2, None, ALU.bitwise_and)
                        if layer == 1:
                            nc.vector.tensor_copy(
                                h_sb[:, of_group(c), 0:F].rearrange("p (b k) f -> p b k f", b=2),
                                uh_banks[k][:, :, :, 0:F])
                        nc.vector.tensor_copy(uv[:, of_group(c), :].rearrange("p (b k) c -> p b k c", b=2),
                                              uh_banks[k][:, :, :, cols0(layer):cols0(layer) + 2])\
                            .then_inc(u_copied, 1)
                dve.wait_ge(u_copied, FREE + (layer + 1) * GROUPS)
                dve.wait_ge(h_copied, 1)
                nc.vector.reduce_max(vmax_part[:, :], uv[:, :, 1], AX.X)
                nc.vector.reduce_sum(hsum_part[:, :], h_sb[:, :, :].rearrange("p b f -> p f b"), AX.X)\
                    .then_inc(stat_in, 1)
                dve.wait_ge(stat_out, 2 * layer + 1)
                nc.vector.tensor_copy(hsum[:, :], acc[:, 7, 0:FE])
                nc.vector.reduce_max(vmax_one[:, :], acc[0:1, 6, 0:P], AX.X).then_inc(stat_in, 1)
                dve.wait_ge(stat_out, 2 * layer + 2)
                nc.vector.tensor_copy(vmax[:, :], acc[:, 6, P:P + 1]).then_inc(acc_free, 2)
                dve.wait_ge(acc_free, layer * LAYER_FREES + 2)
                ts(v_huge[:, :], uv[:, :, 1], HUGE, 2.0 ** -30, ALU.mult, ALU.add)
                ts(fac[:, 0, :], uv[:, :, 0], vmax[:, :], None, ALU.add)
                ts(fac[:, 1, :], uv[:, :, 0], vmax[:, :], SLOPES[layer], ALU.add, ALU.mult)
                ts(fac[:, 2, :], uv[:, :, 1], vmax[:, :], None, ALU.subtract)
                link(ts(fac[:, 3, :], uv[:, :, 1], vmax[:, :], SLOPES[layer], ALU.subtract, ALU.mult))
                link(tt(peak[:, :], fac[:, 0, :], fac[:, 1, :], ALU.max))
                v_bits = v_huge[:, :].bitcast(INT32)
                ts(v_bits, v_bits, 1, None, ALU.bitwise_or)
                tt(fac[:, 0, :], fac[:, 0, :], peak[:, :], ALU.subtract)
                tt(fac[:, 1, :], fac[:, 1, :], peak[:, :], ALU.subtract).then_inc(exp_in, 1)
                dve.wait_ge(exp_out, layer + 1)

            def split(layer, pair):
                for k, buffer in enumerate((stage, stage_2)):
                    blocks = of_group(2 * pair + k)
                    dve.wait_ge(parts_ready, FREE + layer * GROUPS + max(2 * pair + k - 1, 0))
                    tt(buffer[:, :, 0, :], h_sb[:, blocks, :], wide(fac[:, 2, blocks], FE), ALU.mult)
                    tt(buffer[:, :, 1, :], h_sb[:, blocks, :], wide(fac[:, 3, blocks], FE), ALU.mult)\
                        .then_inc(stage_filled, 1)
                for part in range(PARTS - 1):
                    for k, buffer in enumerate((stage, stage_2)):
                        rounded = hs_sb[:, of_group(2 * pair + k), :, part, :]
                        dve.wait_ge(part_made, 2 * (PARTS - 1) * (layer * GROUPS // 2 + pair) + 2 * part + k + 1)
                        tt(buffer[:, :, :, :], buffer[:, :, :, :], rounded, ALU.subtract).then_inc(stage_filled, 1)

            def masks(layer, g, q, k):
                t = layer * LB + g * BATCHES + q * UNROLL + k
                adj = adj_sb[:, k, :, :].bitcast(INT16)
                kind = sign_sb[:, k, :, :].bitcast(INT16)
                dve.wait_ge(adj_loaded[k], 16 * (layer * LB // UNROLL + g * QUADS + q + 1))
                dve.wait_ge(sign_ready, t + 1)
                tt(kind, adj, sign_sb[:, k, :, :].bitcast(UINT16), ALU.min).then_inc(adj_read, 1)
                dve.wait_ge(adj_read, t + 1)
                dve.wait_ge(masks_used, t + 1 + S2_SLOTS - S1_SLOTS)
                ts(s1_sb[:, k % S1_SLOTS, :, :], kind, float(PLUS_BITS), None, ALU.is_equal)
                ts(s2_sb[:, k, :, :], kind, float(PLUS_BITS), None, ALU.is_gt).then_inc(masks_ready, 1)

            def add_parts(layer, g):
                for half in range(2):
                    banks = slice(half * HALF, (half + 1) * HALF)
                    dve.wait_ge(first_copied, 2 * (layer * GROUPS + g) + half + 1)
                    step = layer * GROUPS * 2 + 2 * g + half
                    tt(stage[:, banks, :, :], stage[:, banks, :, :], sums[:, banks, :, 1, :], ALU.add)\
                        .then_inc(mid_added, 1)
                    dve.wait_ge(mid_added, step + 1)
                    tt(stage[:, banks, :, :], stage[:, banks, :, :], sums[:, banks, :, 2, :], ALU.add)\
                        .then_inc(acc_free, 1)

            def attend(layer, g, base):
                rows = of_group(g)
                dve.wait_ge(acc_free, layer * LAYER_FREES + 2 + 2 * (g + 1))
                dve.wait_ge(rows_ready, FREE + layer * GROUPS + g)
                tt(num, stage[:, :, 0, :], wide(fac[:, 0, rows], FE), ALU.mult)
                link(tt(tmp, stage[:, :, 1, :], wide(fac[:, 1, rows], FE), ALU.mult), base)
                tt(num, num, tmp, ALU.add).then_inc(stage_read, 1)
                dve.wait_ge(stage_read, FREE + layer * GROUPS + g + 1)
                link(ts(small[:, 0, :], num[:, :, F], 0.0, None, ALU.is_equal), base)
                link(tt(tmp, wide(hsum[:, :], FE, 1), wide(small[:, 0, :], FE), ALU.mult), base)
                link(tt(num, num, tmp, ALU.add), base)
                link(nc.vector.reciprocal(small[:, 1, :], num[:, :, F]), base)
                link(tt(tmp[:, :, 0:F], num[:, :, 0:F], wide(small[:, 1, :], F), ALU.mult), base)
                y, o = num[:, :, 0:F], tmp[:, :, 0:F]
                if layer == 0:
                    link(stt(y, o, 0.0, x_sb[:, rows, :], ALU.max, ALU.add), base)
                else:
                    ts(y, o, 0.0, None, ALU.min).then_inc(elu_in, 1)

            def residual(layer, g, base):
                rows = of_group(g)
                y, o = num[:, :, 0:F], tmp[:, :, 0:F]
                if layer == 1:
                    dve.wait_ge(elu_out, g + 1)
                    link(stt(y, o, 0.0, y, ALU.max, ALU.add), base)
                    link(stt(y, y, -1.0, x_sb[:, rows, :], ALU.add, ALU.add), base)
                link(nc.vector.reduce_sum(small[:, 0, :], y, AX.X), base)
                link(ts(small[:, 1, :], small[:, 0, :], 1.0 / F, None, ALU.mult), base)
                link(tt(y, y, wide(small[:, 1, :], F), ALU.subtract), base)
                link(tt(o, y, y, ALU.mult), base)
                link(nc.vector.reduce_sum(small[:, 0, :], o, AX.X), base)
                ts(small[:, 2, :], small[:, 0, :], 1.0 / F, EPS, ALU.mult, ALU.add).then_inc(norm_in, 1)

            def normalise(layer, g, base):
                root, t = small[:, 3, :], small[:, 4, :]
                dve.wait_ge(norm_out, layer * GROUPS + g + 1)
                link(tt(t, root, root, ALU.mult), base)
                link(tt(t, t, small[:, 2, :], ALU.mult), base)
                link(ts(t, t, -0.5, 1.5, ALU.mult, ALU.add), base)
                link(tt(small[:, 5, :], root, t, ALU.mult), base)
                tt(x_sb[:, of_group(g), :], num[:, :, 0:F], wide(small[:, 5, :], F), ALU.mult)\
                    .then_inc(rows_ready, 1)

            for layer in range(2):
                if layer == 1:
                    dve.wait_ge(rows_ready, FREE + GROUPS)
                    dve.wait_ge(masks_used, S2_SLOTS + LB)
                    dve.wait_ge(sign_ready, LB)
                prepare(layer)
                split(layer, 0)
                for q in range(QUADS):
                    masks(layer, 0, q, 0)
                    masks(layer, 0, q, 1)
                    if q < QUADS - 1:
                        split(layer, q + 1)
                    masks(layer, 0, q, 2)
                    masks(layer, 0, q, 3)
                start, steps = count[0], FINISH_STEPS[layer]
                with dve.Fori(1, GROUPS) as g:
                    base = (g - 1) * steps
                    masks(layer, g, 0, 0)
                    add_parts(layer, g - 1)
                    masks(layer, g, 0, 1)
                    attend(layer, g - 1, base)
                    masks(layer, g, 0, 2)
                    residual(layer, g - 1, base)
                    masks(layer, g, 0, 3)
                    normalise(layer, g - 1, base)
                    with dve.Fori(1, QUADS) as q:
                        for k in range(UNROLL):
                            masks(layer, g, q, k)
                assert count[0] - start == steps
                count[0] = start + (GROUPS - 1) * steps
                add_parts(layer, GROUPS - 1)
                attend(layer, GROUPS - 1, 0)
                residual(layer, GROUPS - 1, 0)
                normalise(layer, GROUPS - 1, 0)
    return nc


def kernel(x, adj, L0_gnn_a, L1_gnn_W, L1_gnn_a):
    import concourse.bacc as bacc
    from concourse.bass_utils import run_bass_kernel_spmd

    x, adj, a0, w, a1 = (np.asarray(v) for v in (x, adj, L0_gnn_a, L1_gnn_W, L1_gnn_a))
    adj_t = adj.reshape(GROUPS, GN, BATCHES, JB, P).transpose(0, 2, 4, 3, 1)
    arrays = {
        "x_rows": x.reshape(BLOCKS, P, F).transpose(1, 0, 2),
        "x_cols": x.T,
        "adj_t": adj_t.reshape(GROUPS * BATCHES * P, JB * GN),
        "a0": a0.reshape(2, F).T,
        "a1": a1.reshape(2, F).T,
        "w": w,
        "w_t": w.T,
    }
    arrays = {name: np.ascontiguousarray(v) for name, v in arrays.items()}
    nc = bacc.Bacc("TRN2", target_bir_lowering=False, num_devices=1)
    args = [nc.dram_tensor(name, v.shape, mybir.dt.from_np(v.dtype), kind="ExternalInput").ap()
            for name, v in arrays.items()]
    out = nc.dram_tensor("out", (P, BLOCKS, F), FP32, kind="ExternalOutput").ap()
    build(nc, *args, out)
    result = run_bass_kernel_spmd(nc, [arrays], core_ids=[0]).results[0]["out"]
    return result.transpose(1, 0, 2).reshape(N, F)
```

```python
import numpy as np
import concourse.bass as bass
from concourse import mybir
from contextlib import ExitStack

FP32 = mybir.dt.float32
BF16 = mybir.dt.bfloat16
FP16 = mybir.dt.float16
INT16 = mybir.dt.int16
UINT16 = mybir.dt.uint16
INT32 = mybir.dt.int32
ALU = mybir.AluOpType
ACT = mybir.ActivationFunctionType
AX = mybir.AxisListType

P = 128
N = 8192
F = 64
FE = F + 1
BLOCKS = N // P
GROUPS = 8
GB = BLOCKS // GROUPS
GN = GB * P
JB = 4
BATCHES = BLOCKS // JB
UNROLL = 4
QUADS = BATCHES // UNROLL
CONSTS = 8 * 16
PARTS_PER_QUAD = GROUPS // QUADS
PARTS = 3
HALF = GB // 2
BANK = 512
HUGE = 2.0 ** 100
PLUS_BITS = 0x3C00
EPS = 1e-5
SLOPES = (0.2, 0.01)
ADJ_SLOTS, S1_SLOTS, S2_SLOTS = 4, 2, 4
SLOTS = (S1_SLOTS, S2_SLOTS)
LB = GROUPS * BATCHES
LAYER_FREES = 2 + 2 * GROUPS
U_PAIRS = (3, 2)
FIND_PEAK_AFTER = 3
SPREAD_PEAK_AFTER = 4
SIGNS_AFTER_U = GROUPS - 4
EARLY = 2
EARLY_PER_COPY = -(-EARLY * JB // (GROUPS - 2))
WORDS = BLOCKS * PARTS * FE
ROOT_AFTER_XT = 5
SUM_AFTER = 0
ELU_AFTER, ROOT_AFTER = 9, 14
FLAG_AFTER = 4
FREE = 1
FINISH_STEPS = (12, 13)
COMBINE_STEPS = 2


def build(nc, x_rows, x_cols, adj_t, a0_row, a0, a1, w, w_t, out):
    ctx = ExitStack()

    def sb(name, shape, dt=FP32):
        return ctx.enter_context(nc.sbuf_tensor(name, shape, dt))

    def sem(name):
        return ctx.enter_context(nc.semaphore(name))

    with ctx:
        x_sb = sb("x_sb", [P, BLOCKS, F])
        h_sb = sb("h_sb", [P, BLOCKS, FE])
        hs_flat = sb("hs_flat", [P, BLOCKS * 2 * PARTS * FE], BF16)
        hs_sb = hs_flat[:, :].rearrange("p (b s t f) -> p b s t f", b=BLOCKS, s=2, t=PARTS)
        u_row = sb("u_row", [P, N])
        adj_sb = sb("adj_sb", [P, ADJ_SLOTS, JB, GN], BF16)
        sign_sb = sb("sign_sb", [P, S2_SLOTS, JB, GN], FP16)
        s1_sb = sb("s1_sb", [P, S1_SLOTS, JB, GN], BF16)
        s2_sb = sign_sb[:, :, :, :].bitcast(BF16)
        stage = sb("stage", [P, GB, 2, FE])
        stage_2 = sb("stage_2", [P, GB, 2, FE])
        num = stage_2[:, :, 0, :]
        tmp = stage_2[:, :, 1, :]
        words = hs_flat[:, :].bitcast(FP32)
        xt_sb = words[:, WORDS - N // 2:WORDS].rearrange("p (c n) -> p c n", c=GROUPS)
        product = words[:, 0:N // 2].rearrange("p (b f) -> p b f", b=BLOCKS)
        hsum_group = words[:, N // 2:N // 2 + GROUPS * FE].rearrange("p (c f) -> p c f", c=GROUPS)
        product_u = sign_sb[:, 2:4, :, :].rearrange("p k j i -> p (k j i)").bitcast(FP32)\
            .rearrange("p (b f) -> p b f", b=BLOCKS)
        hsum_half = words[:, N // 2:N // 2 + BLOCKS // 2 * FE].rearrange("p (b f) -> p b f", f=FE)
        ident = sb("ident", [P, P])
        ones = sb("ones", [P, P])
        columns = sb("columns", [P, 2])
        vmax_part, vmax = columns[:, 0:1], columns[:, 1:2]
        a_row = sb("a_row", [P, 2, F])
        a0_sb = sb("a0_sb", [P, 2])
        w_ext = sb("w_ext", [P, F + 2])
        w_pair = sb("w_pair", [P, 2, F + 2])
        a_wide = [sb("a0_wide", [P, P]), sb("a1_wide", [P, P])]
        a1_sb = sb("a1_sb", [F, 2])
        w_t_sb = sb("w_t_sb", [F, 2, F])
        uv = sb("uv", [P, BLOCKS, 2])
        v_huge = sb("v_huge", [P, BLOCKS])
        fac = sb("fac", [P, 4, BLOCKS])
        peak = sb("peak", [P, BLOCKS])
        vmax_one = sb("vmax_one", [1, 1])
        hsum_part = sb("hsum_part", [P, FE])
        hsum = sb("hsum", [P, FE])
        small = sb("small", [P, 6, GB])
        acc = ctx.enter_context(nc.psum_tensor("acc", [P, GB, BANK], FP32))

        consts_loaded = sem("consts_loaded")
        x_loaded = sem("x_loaded")
        xt_loaded = sem("xt_loaded")
        ident_made = sem("ident_made")
        adj_loaded = [sem(f"adj_loaded{i}") for i in range(ADJ_SLOTS)]
        w_projected = sem("w_projected")
        w_ready = sem("w_ready")
        xt_made = sem("xt_made")
        xt_copied = sem("xt_copied")
        u_made = sem("u_made")
        h_made = sem("h_made")
        v_ready = sem("v_ready")
        u_cleared = sem("u_cleared")
        u_copied = sem("u_copied")
        h_copied = sem("h_copied")
        h_summed = sem("h_summed")
        hsum_made = sem("hsum_made")
        pool_step = sem("pool_step")
        ones_made = sem("ones_made")
        u_by_node = sem("u_by_node")
        stat_in = sem("stat_in")
        stat_out = sem("stat_out")
        exp_in = sem("exp_in")
        exp_out = sem("exp_out")
        vector_step = sem("vector_step")
        parts_ready = sem("parts_ready")
        products_made = sem("products_made")
        combine_step = sem("combine_step")
        alone_found = sem("alone_found")
        combined = sem("combined")
        stage_filled = sem("stage_filled")
        part_made = sem("part_made")
        sign_ready = sem("sign_ready")
        adj_read = sem("adj_read")
        masks_ready = sem("masks_ready")
        masks_used = sem("masks_used")
        half_summed = sem("half_summed")
        first_copied = sem("first_copied")
        acc_free = sem("acc_free")
        mid_added = sem("mid_added")
        stage_read = sem("stage_read")
        elu_in = sem("elu_in")
        elu_out = sem("elu_out")
        norm_in = sem("norm_in")
        norm_ln = sem("norm_ln")
        norm_out = sem("norm_out")
        rows_ready = sem("rows_ready")
        out_sent = sem("out_sent")
        block = ctx.enter_context(nc.Block())

        def of_group(g):
            return bass.ds(g * GB, GB)

        sums = acc[:, :, 0:2 * PARTS * FE].rearrange("p b (s t f) -> p b s t f", s=2, t=PARTS)
        def u_banks(layer, c):
            first = 2 + 2 * (c % U_PAIRS[layer])
            return acc[:, first:first + 2, :]

        h_banks = acc[:, 6:8, 0:HALF * (F + 2)].rearrange("p m (b c) -> p m b c", b=HALF)

        def wide(ap, n, dim=2):
            return ap.unsqueeze(dim).to_broadcast([P, GB, n])

        def multiply(engine, layer, pair):
            for k, buffer in enumerate((stage, stage_2)):
                blocks = of_group(2 * pair + k)
                engine.wait_ge(parts_ready, FREE + layer * GROUPS + max(2 * pair + k - 1, 0))
                engine.tensor_tensor(buffer[:, :, 0, :], h_sb[:, blocks, :], wide(fac[:, 2, blocks], FE), ALU.mult)
                engine.tensor_tensor(buffer[:, :, 1, :], h_sb[:, blocks, :], wide(fac[:, 3, blocks], FE), ALU.mult)\
                    .then_inc(products_made, 1)

        @block.gpsimd
        def _(pool):
            pool.memset(ident[:, :], 0.0).then_inc(ident_made, 1)
            pool.wait_ge(ident_made, 1)
            pool.affine_select(out=ident[:, :], in_=ident[:, :], compare_op=ALU.not_equal, fill=1.0,
                               base=0, pattern=[[-1, P]], channel_multiplier=1).then_inc(ident_made, 1)

            def load(batch, k):
                pool.dma_start(adj_sb[:, k, :, :].rearrange("p j i -> p (j i)"),
                               adj_t[bass.ds(batch * P, P), :]).then_inc(adj_loaded[k], 16)

            def combine(layer, g):
                rows, base = of_group(g), (layer * (GROUPS - 1) + g) * COMBINE_STEPS
                pool.wait_ge(acc_free, layer * LAYER_FREES + 2 + 2 * (g + 1))
                pool.wait_ge(rows_ready, FREE + layer * GROUPS + g)
                pool.tensor_tensor(num, stage[:, :, 0, :], wide(fac[:, 0, rows], FE), ALU.mult)
                pool.tensor_tensor(tmp, stage[:, :, 1, :], wide(fac[:, 1, rows], FE), ALU.mult)\
                    .then_inc(combine_step, 1)
                pool.wait_ge(combine_step, base + 1)
                pool.tensor_tensor(num, num, tmp, ALU.add).then_inc(stage_read, 1)

            def add_mean(layer, g):
                done = layer * (GROUPS - 1) + g
                pool.wait_ge(alone_found, done + 1)
                pool.tensor_tensor(tmp, wide(hsum[:, :], FE, 1), wide(small[:, 0, :], FE), ALU.mult)\
                    .then_inc(combine_step, 1)
                pool.wait_ge(combine_step, done * COMBINE_STEPS + 2)
                pool.tensor_tensor(num, num, tmp, ALU.add).then_inc(combined, 1)

            def load_quad(layer, q, pieces={}, finish=None):
                for k in range(UNROLL):
                    if k in pieces:
                        pieces[k](layer, finish)
                    pool.wait_ge(adj_read, layer * LB + q * UNROLL + k + 1 - ADJ_SLOTS)
                    load(q * UNROLL + k, k)

            pool.wait_ge(x_loaded, 16)
            pool.wait_ge(xt_loaded, 16)
            for layer in range(2):
                if layer == 0:
                    for k in range(ADJ_SLOTS):
                        load(k, k)
                    pool.wait_ge(h_copied, 1)
                    pool.wait_ge(ones_made, 2)
                    n, upper, lower = BLOCKS // 2, h_sb[:, 0:BLOCKS // 2, :], h_sb[:, BLOCKS // 2:BLOCKS, :]
                    while n > 1:
                        pool.tensor_tensor(hsum_half[:, 0:n, :], upper, lower, ALU.add).then_inc(pool_step, 1)
                        n //= 2
                        upper, lower = hsum_half[:, 0:n, :], hsum_half[:, n:2 * n, :]
                        pool.wait_ge(pool_step, (BLOCKS // 2 // n).bit_length() - 1)
                    pool.tensor_tensor(hsum_part[:, :].unsqueeze(1), upper, lower, ALU.add).then_inc(h_summed, 1)
                    step = (BLOCKS // 2).bit_length() - 1
                    pool.tensor_tensor(product_u, x_sb[:, :, :], a_row[:, 0, :].unsqueeze(1).to_broadcast(
                        [P, BLOCKS, F]), ALU.mult).then_inc(pool_step, 1)
                    n = F
                    while n > 2:
                        n //= 2
                        step += 1
                        pool.wait_ge(pool_step, step)
                        pool.tensor_tensor(product_u[:, :, 0:n], product_u[:, :, 0:n], product_u[:, :, n:2 * n],
                                           ALU.add).then_inc(pool_step, 1)
                    pool.wait_ge(pool_step, step + 1)
                    pool.tensor_tensor(uv[:, :, 0:1], product_u[:, :, 0:1], product_u[:, :, 1:2], ALU.add)\
                        .then_inc(u_by_node, 1)
                for q in range(1 - layer, QUADS):
                    if q == 1:
                        pool.wait_ge(exp_out, 2 * layer + 1)
                    if q >= 1:
                        multiply(pool, layer, q)
                    load_quad(layer, q)
                with pool.Fori(1, GROUPS) as g:
                    load_quad(layer, g * QUADS)
                    load_quad(layer, g * QUADS + 1, {2: combine}, g - 1)
                    load_quad(layer, g * QUADS + 2, {1: add_mean}, g - 1)
                    load_quad(layer, g * QUADS + 3)

        @block.sync
        def _(sp):
            for half in range(2):
                rows = slice(half * F, (half + 1) * F)
                sp.dma_start(a0_sb[rows, :], a0).then_inc(consts_loaded, 16)
                sp.dma_start(w_ext[rows, 0:F], w).then_inc(consts_loaded, 16)
                sp.dma_start(w_t_sb[:, half, :], w_t).then_inc(consts_loaded, 16)
            sp.dma_start(a1_sb[:, :], a1).then_inc(consts_loaded, 16)
            sp.dma_start(a_row[:, :, :].rearrange("p k f -> p (k f)"), a0_row.to_broadcast([P, 2 * F]))\
                .then_inc(consts_loaded, 16)
            sp.dma_start(x_sb[:, :, :], x_rows).then_inc(x_loaded, 16)
            with sp.Fori(0, GROUPS) as g:
                sp.wait_ge(rows_ready, FREE + GROUPS + g + 1)
                sp.dma_start(out[:, of_group(g), :], x_sb[:, of_group(g), :]).then_inc(out_sent, 16)
            sp.wait_ge(out_sent, 16 * GROUPS)

        @block.tensor
        def _(pe):
            pe.sem_inc(masks_used, S2_SLOTS)
            pe.wait_ge(consts_loaded, CONSTS)
            nc.tensor.matmul(acc[:, 7, 0:2], w_t_sb[:, :, :].rearrange("k r m -> k (r m)"), a1_sb[:, :],
                             start=True, stop=True).then_inc(w_projected, 1)
            pe.wait_ge(w_ready, 1)
            pe.wait_ge(ident_made, 2)

            def project_u(layer, c):
                for half in range(2):
                    rows = slice(half * F, (half + 1) * F)
                    ins = nc.tensor.matmul(u_banks(layer, c)[:, half, :], a_wide[layer][rows, :],
                                           xt_sb[rows, c, :], start=True, stop=True)
                ins.then_inc(u_made, 1)

            def transpose(c):
                pe.wait_ge(rows_ready, FREE + c + 1)
                for m in range(HALF):
                    ins = nc.tensor.transpose(
                        acc[:, c % 2, m * P:(m + 1) * P],
                        x_sb[:, c * GB + 2 * m:c * GB + 2 * m + 2, :].rearrange("p b f -> p (b f)"), ident[:, :])
                ins.then_inc(xt_made, 1)

            def project_h(c):
                for m in range(HALF):
                    ins = nc.tensor.matmul(
                        h_banks[:, m // 2, 2 * (m % 2):2 * (m % 2) + 2, :].rearrange("p b c -> p (b c)"),
                        xt_sb[:, c, m * P:(m + 1) * P], w_pair[:, :, :].rearrange("p b c -> p (b c)"),
                        start=True, stop=True)
                ins.then_inc(h_made, 1)

            def find_peak(layer):
                pe.wait_ge(stat_in, 2 * layer + 1)
                nc.tensor.transpose(acc[0:1, 0, 0:P], vmax_part[:, :], ident[:, :]).then_inc(stat_out, 1)

            def spread_peak(layer):
                pe.wait_ge(stat_in, 2 * layer + 2)
                nc.tensor.matmul(acc[:, 0, P:P + 1], ones[0:1, :], vmax_one[:, :], start=True, stop=True)\
                    .then_inc(stat_out, 1)

            def prepare(layer):
                if layer == 0:
                    pe.wait_ge(xt_loaded, 16)
                    for c in range(GROUPS):
                        if c >= U_PAIRS[0]:
                            pe.wait_ge(u_copied, c + 1 - U_PAIRS[0])
                        project_u(layer, c)
                        if c == FIND_PEAK_AFTER:
                            find_peak(layer)
                        if c == SPREAD_PEAK_AFTER:
                            spread_peak(layer)
                else:
                    pe.wait_ge(acc_free, LAYER_FREES)
                    transpose(0)
                    transpose(1)
                    for c in range(GROUPS):
                        pe.wait_ge(xt_copied, c + 1)
                        if c >= 2:
                            pe.wait_ge(u_copied, GROUPS + c - 1)
                        project_u(layer, c)
                        if c >= 1:
                            pe.wait_ge(h_copied, 1 + c)
                        project_h(c)
                        if c + 2 < GROUPS:
                            transpose(c + 2)
                    find_peak(layer)
                    spread_peak(layer)
                pe.wait_ge(h_summed, layer + 1)
                nc.tensor.matmul(acc[:, 1, 0:FE], ones[:, :], hsum_part[:, :], start=True, stop=True)\
                    .then_inc(hsum_made, 1)
                pe.wait_ge(u_copied, (layer + 1) * GROUPS)

            def quad(layer, g, q, first=False, last=False):
                for k in range(UNROLL):
                    batch = q * UNROLL + k
                    if k % 2 == 0:
                        pe.wait_ge(parts_ready, FREE + layer * GROUPS + PARTS_PER_QUAD * q + k // 2 + 1)
                    pe.wait_ge(masks_ready, layer * LB + g * BATCHES + batch + 1)
                    for b in range(GB):
                        if first and k == 0 and b % HALF == 0:
                            pe.wait_ge(acc_free, layer * LAYER_FREES + 2 * g + 1 + b // HALF)
                        for j in range(JB):
                            for s, mask in enumerate((s1_sb, s2_sb)):
                                ins = nc.tensor.matmul(
                                    acc[:, b, s * PARTS * FE:(s + 1) * PARTS * FE],
                                    mask[:, k % SLOTS[s], j, b * P:(b + 1) * P],
                                    hs_sb[:, bass.ds(batch * JB + j, 1), s, :, :].rearrange(
                                        "p o t f -> p (o t f)"),
                                    start=first and k == 0 and j == 0 and s == 0,
                                    stop=last and k == UNROLL - 1 and j == JB - 1 and s == 1,
                                    skip_group_check=True)
                        if last and k == UNROLL - 1 and b == HALF - 1:
                            ins.then_inc(half_summed, 1)
                    ins.then_inc(masks_used, 1)

            for layer in range(2):
                prepare(layer)
                with pe.Fori(0, GROUPS) as g:
                    quad(layer, g, 0, first=True)
                    with pe.Fori(1, QUADS - 1) as q:
                        quad(layer, g, q)
                    quad(layer, g, QUADS - 1, last=True)

        @block.scalar
        def _(act):
            def sign_block(layer, g, batch, j):
                ins = nc.scalar.activation(
                    sign_sb[:, batch % S2_SLOTS, j, :],
                    u_row[:, bass.ds((g + batch) * GN - batch * GN, GN)], ACT.Sign,
                    bias=v_huge[:, batch * JB + j:batch * JB + j + 1])
                if j == JB - 1:
                    ins.then_inc(sign_ready, 1)

            def sign(layer, g, batch):
                act.wait_ge(masks_used, layer * LB + g * BATCHES + batch + 1)
                for j in range(JB):
                    sign_block(layer, g, batch, j)

            def keep_u(layer, c):
                act.wait_ge(u_made, layer * GROUPS + c + 1)
                nc.scalar.copy(u_row[:, c * GN:(c + 1) * GN].rearrange("p (m r n) -> p r m n", m=HALF, r=2),
                               u_banks(layer, c).rearrange("p r (m n) -> p r m n", m=HALF)).then_inc(u_copied, 1)

            def round_parts(layer, pair, part):
                for k, buffer in enumerate((stage, stage_2)):
                    done = layer * GROUPS // 2 + pair
                    if part == 0:
                        act.wait_ge(products_made, 2 * done + k + 1)
                    else:
                        act.wait_ge(stage_filled, 2 * (PARTS - 1) * done + 2 * (part - 1) + k + 1)
                    nc.scalar.copy(hs_sb[:, of_group(2 * pair + k), :, part, :], buffer[:, :, :, :])\
                        .then_inc(part_made if part < PARTS - 1 else parts_ready, 1)

            def copy_first(layer, g):
                done = layer * GROUPS + g
                act.wait_ge(stage_read, FREE + done)
                for half in range(2):
                    if half == 0:
                        act.wait_ge(half_summed, done + 1)
                    else:
                        act.wait_ge(masks_used, S2_SLOTS + layer * LB + (g + 1) * BATCHES)
                    banks = slice(half * HALF, (half + 1) * HALF)
                    nc.scalar.copy(stage[:, banks, :, :], sums[:, banks, :, 0, :]).then_inc(first_copied, 1)

            def elu_exp(g):
                act.wait_ge(elu_in, g + 1)
                nc.scalar.activation(num[:, :, 0:F], num[:, :, 0:F], ACT.Exp).then_inc(elu_out, 1)

            def norm_root(layer, g):
                done = layer * GROUPS + g
                act.wait_ge(norm_in, done + 1)
                nc.scalar.activation(small[:, 3, :], small[:, 2, :], ACT.Ln).then_inc(norm_ln, 1)
                act.wait_ge(norm_ln, done + 1)
                nc.scalar.activation(small[:, 3, :], small[:, 3, :], ACT.Exp, scale=-0.5).then_inc(norm_out, 1)

            for layer in range(2):
                if layer == 0:
                    act.dma_start(xt_sb, x_cols).then_inc(xt_loaded, 16)
                    act.wait_ge(x_loaded, 16)
                    nc.scalar.copy(h_sb[:, :, 0:F], x_sb[:, :, :]).then_inc(h_copied, 1)
                else:
                    early = [(batch, j) for batch in range(EARLY) for j in range(JB)]
                    act.wait_ge(sign_ready, LB)
                    for c in range(GROUPS + 1):
                        if c < GROUPS:
                            act.wait_ge(xt_made, c + 1)
                            nc.scalar.copy(xt_sb[:, c, :], acc[:, c % 2, :]).then_inc(xt_copied, 1)
                        if c >= 1:
                            keep_u(1, c - 1)
                        if c == ROOT_AFTER_XT:
                            norm_root(0, GROUPS - 1)
                        if c == 3:
                            act.wait_ge(v_ready, 3)
                            act.wait_ge(u_cleared, 3)
                            act.wait_ge(masks_used, LB + S2_SLOTS)
                        if c >= 3:
                            for batch, j in early[:EARLY_PER_COPY]:
                                sign_block(1, 0, batch, j)
                            early = early[EARLY_PER_COPY:]
                if layer == 0:
                    for c in range(SIGNS_AFTER_U + 1):
                        keep_u(0, c)
                    act.wait_ge(v_ready, 2)
                    act.wait_ge(u_cleared, 1)
                    act.wait_ge(masks_used, 1)
                    sign_block(0, 0, 0, 0)
                act.wait_ge(exp_in, 2 * layer + 1)
                nc.scalar.activation(fac[:, 2:4, :], fac[:, 2:4, :], ACT.Exp).then_inc(exp_out, 1)
                for part in range(PARTS):
                    if part == 0 and layer == 0:
                        sign_block(0, 0, 0, 1)
                    round_parts(layer, 0, part)
                    if part == 0 and layer == 0:
                        sign_block(0, 0, 0, 2)
                        sign_block(0, 0, 0, 3)
                        keep_u(0, GROUPS - 3)
                    if part == 1 and layer == 0:
                        keep_u(0, GROUPS - 2)
                        keep_u(0, GROUPS - 1)
                for batch in range(BATCHES):
                    q, k = divmod(batch, UNROLL)
                    if batch == 2 and layer == 0:
                        act.wait_ge(u_by_node, 1)
                    if batch >= (1 if layer == 0 else EARLY):
                        sign(layer, 0, batch)
                    if q < QUADS - 1 and k > 0:
                        round_parts(layer, q + 1, k - 1)
                act.wait_ge(exp_in, 2 * layer + 2)
                nc.scalar.activation(fac[:, 0:2, :], fac[:, 0:2, :], ACT.Exp).then_inc(exp_out, 1)
                act.wait_ge(u_cleared, 2 * layer + 2)
                with act.Fori(1, GROUPS) as g:
                    for batch in range(BATCHES):
                        sign(layer, g, batch)
                        if batch == SUM_AFTER + 1:
                            copy_first(layer, g - 1)
                        if batch == ELU_AFTER and layer == 1:
                            elu_exp(g - 1)
                        if batch == ROOT_AFTER:
                            norm_root(layer, g - 1)
                copy_first(layer, GROUPS - 1)
                if layer == 1:
                    elu_exp(GROUPS - 1)
                    norm_root(layer, GROUPS - 1)

        @block.vector
        def _(dve):
            count = [0]

            def link(ins, base=None):
                count[0] += 1
                ins.then_inc(vector_step, 1)
                dve.wait_ge(vector_step, count[0] if base is None else base + count[0])

            tt, ts, stt = nc.vector.tensor_tensor, nc.vector.tensor_scalar, nc.vector.scalar_tensor_tensor

            for free in (stage_read, parts_ready, rows_ready):
                dve.sem_inc(free, FREE)
            nc.vector.memset(ones[:, :], 1.0)
            nc.vector.memset(w_pair[:, :, :], 0.0).then_inc(ones_made, 1)
            nc.vector.memset(h_sb[:, :, F:FE], 1.0).then_inc(ones_made, 1)
            dve.wait_ge(consts_loaded, CONSTS)
            ts(a_wide[0][:, :], a0_sb[:, 0:1].to_broadcast([P, P]), HUGE, None, ALU.mult)
            dve.wait_ge(w_projected, 1)
            link(nc.vector.tensor_copy(w_ext[:, F:F + 2], acc[:, 7, 0:2]))
            dve.wait_ge(ones_made, 1)
            for half in range(2):
                rows = slice(half * F, (half + 1) * F)
                nc.vector.tensor_copy(w_pair[rows, half, :], w_ext[rows, :])
            ts(a_wide[1][:, :], w_ext[:, F:F + 1].to_broadcast([P, P]), HUGE, None, ALU.mult).then_inc(w_ready, 1)

            def clear_u(layer, first, last):
                dve.wait_ge(u_copied, layer * GROUPS + last)
                bits = u_row[:, first * GN:last * GN].bitcast(INT32)
                ts(bits, bits, -2, None, ALU.bitwise_and).then_inc(u_cleared, 1)

            def lift_v(blocks):
                link(ts(v_huge[:, blocks], uv[:, blocks, 1], HUGE, 2.0 ** -30, ALU.mult, ALU.add))
                v_bits = v_huge[:, blocks].bitcast(INT32)
                ts(v_bits, v_bits, 1, None, ALU.bitwise_or).then_inc(v_ready, 1)

            def keep_h(c):
                blocks = of_group(c)
                dve.wait_ge(h_made, c + 1)
                nc.vector.tensor_copy(uv[:, blocks, :].rearrange("p (m b) c -> p m b c", m=2),
                                      h_banks[:, :, :, F:F + 2])
                nc.vector.tensor_copy(h_sb[:, blocks, 0:F].rearrange("p (m b) c -> p m b c", m=2),
                                      h_banks[:, :, :, 0:F]).then_inc(h_copied, 1)

            def sum_h(c):
                link(nc.vector.reduce_sum(hsum_group[:, c, :],
                                          h_sb[:, of_group(c), :].rearrange("p b f -> p f b"), AX.X))

            def prepare(layer):
                if layer == 0:
                    dve.wait_ge(x_loaded, 16)
                    link(tt(product, x_sb[:, :, :], a_row[:, 1, :].unsqueeze(1).to_broadcast([P, BLOCKS, F]),
                            ALU.mult))
                    link(nc.vector.reduce_sum(uv[:, :, 1], product, AX.X))
                    lift_v(slice(0, 2 * GB))
                    lift_v(slice(2 * GB, BLOCKS))
                else:
                    finish = {0: scale, 1: mean_if_alone, 2: divide, 3: centre, 4: variance, 5: normalise}
                    for c in range(GROUPS):
                        if c in finish:
                            finish[c](0, GROUPS - 1, 0)
                        keep_h(c)
                        dve.wait_ge(h_copied, 1 + c + 1)
                        sum_h(c)
                        if c == 1:
                            lift_v(slice(0, 2 * GB))
                            clear_u(1, 0, 1)
                        if c == 6:
                            classify(1, 0, 0)
                    lift_v(slice(2 * GB, BLOCKS))
                nc.vector.reduce_max(vmax_part[:, :], uv[:, :, 1], AX.X).then_inc(stat_in, 1)
                if layer == 0:
                    clear_u(0, 0, 1)
                else:
                    nc.vector.reduce_sum(hsum_part[:, :], hsum_group[:, :, :].rearrange("p c f -> p f c"), AX.X)\
                        .then_inc(h_summed, 1)
                dve.wait_ge(stat_out, 2 * layer + 1)
                nc.vector.reduce_max(vmax_one[:, :], acc[0:1, 0, 0:P], AX.X).then_inc(stat_in, 1)
                if layer == 1:
                    compare(1, 0, 0)
                dve.wait_ge(stat_out, 2 * layer + 2)
                link(nc.vector.tensor_copy(vmax[:, :], acc[:, 0, P:P + 1]))
                ts(fac[:, 2, :], uv[:, :, 1], vmax[:, :], None, ALU.subtract)
                ts(fac[:, 3, :], uv[:, :, 1], vmax[:, :], SLOPES[layer], ALU.subtract, ALU.mult).then_inc(exp_in, 1)
                dve.wait_ge(exp_out, 2 * layer + 1)

            def row_exponents(layer):
                if layer == 0:
                    dve.wait_ge(u_by_node, 1)
                ts(fac[:, 0, :], uv[:, :, 0], vmax[:, :], None, ALU.add)
                link(ts(fac[:, 1, :], uv[:, :, 0], vmax[:, :], SLOPES[layer], ALU.add, ALU.mult))
                link(tt(peak[:, :], fac[:, 0, :], fac[:, 1, :], ALU.max))
                tt(fac[:, 0, :], fac[:, 0, :], peak[:, :], ALU.subtract)
                tt(fac[:, 1, :], fac[:, 1, :], peak[:, :], ALU.subtract).then_inc(exp_in, 1)

            def take_away(layer, pair, part):
                for k, buffer in enumerate((stage, stage_2)):
                    rounded = hs_sb[:, of_group(2 * pair + k), :, part, :]
                    dve.wait_ge(part_made, 2 * (PARTS - 1) * (layer * GROUPS // 2 + pair) + 2 * part + k + 1)
                    tt(buffer[:, :, :, :], buffer[:, :, :, :], rounded, ALU.subtract).then_inc(stage_filled, 1)

            def classify(layer, g, batch):
                t, k = layer * LB + g * BATCHES + batch, batch % ADJ_SLOTS
                adj = adj_sb[:, k, :, :].bitcast(INT16)
                kind = sign_sb[:, k, :, :].bitcast(INT16)
                dve.wait_ge(adj_loaded[k], 16 * (layer * LB // UNROLL + g * QUADS + batch // UNROLL + 1))
                dve.wait_ge(sign_ready, t + 1)
                tt(kind, adj, sign_sb[:, k, :, :].bitcast(UINT16), ALU.min).then_inc(adj_read, 1)

            def compare(layer, g, batch):
                t, k = layer * LB + g * BATCHES + batch, batch % S2_SLOTS
                kind = sign_sb[:, k, :, :].bitcast(INT16)
                dve.wait_ge(adj_read, t + 1)
                dve.wait_ge(masks_used, t + 1 + S2_SLOTS - S1_SLOTS)
                ts(s1_sb[:, batch % S1_SLOTS, :, :], kind, float(PLUS_BITS), None, ALU.is_equal)
                ts(s2_sb[:, k, :, :], kind, float(PLUS_BITS), None, ALU.is_gt).then_inc(masks_ready, 1)

            def add_parts(layer, g, halves=(0, 1)):
                for half in halves:
                    banks = slice(half * HALF, (half + 1) * HALF)
                    dve.wait_ge(first_copied, 2 * (layer * GROUPS + g) + half + 1)
                    step = layer * GROUPS * 2 + 2 * g + half
                    tt(stage[:, banks, :, :], stage[:, banks, :, :], sums[:, banks, :, 1, :], ALU.add)\
                        .then_inc(mid_added, 1)
                    dve.wait_ge(mid_added, step + 1)
                    tt(stage[:, banks, :, :], stage[:, banks, :, :], sums[:, banks, :, 2, :], ALU.add)\
                        .then_inc(acc_free, 1)

            y, o = num[:, :, 0:F], tmp[:, :, 0:F]

            def scale(layer, g, base):
                rows = of_group(g)
                dve.wait_ge(acc_free, layer * LAYER_FREES + 2 + 2 * (g + 1))
                dve.wait_ge(rows_ready, FREE + layer * GROUPS + g)
                tt(num, stage[:, :, 0, :], wide(fac[:, 0, rows], FE), ALU.mult)
                link(tt(tmp, stage[:, :, 1, :], wide(fac[:, 1, rows], FE), ALU.mult), base)
                tt(num, num, tmp, ALU.add).then_inc(stage_read, 1)

            def mean_if_alone(layer, g, base):
                dve.wait_ge(stage_read, FREE + layer * GROUPS + g + 1)
                link(ts(small[:, 0, :], num[:, :, F], 0.0, None, ALU.is_equal), base)
                link(tt(tmp, wide(hsum[:, :], FE, 1), wide(small[:, 0, :], FE), ALU.mult), base)
                link(tt(num, num, tmp, ALU.add), base)

            def divide(layer, g, base):
                link(nc.vector.reciprocal(small[:, 1, :], num[:, :, F]), base)
                link(tt(o, num[:, :, 0:F], wide(small[:, 1, :], F), ALU.mult), base)
                if layer == 0:
                    link(stt(y, o, 0.0, x_sb[:, of_group(g), :], ALU.max, ALU.add), base)
                else:
                    ts(y, o, 0.0, None, ALU.min).then_inc(elu_in, 1)

            def elu(layer, g, base):
                if layer == 1:
                    dve.wait_ge(elu_out, g + 1)
                    link(stt(y, o, 0.0, y, ALU.max, ALU.add), base)
                    link(stt(y, y, -1.0, x_sb[:, of_group(g), :], ALU.add, ALU.add), base)

            def centre(layer, g, base):
                link(nc.vector.reduce_sum(small[:, 0, :], y, AX.X), base)
                link(ts(small[:, 1, :], small[:, 0, :], 1.0 / F, None, ALU.mult), base)
                link(tt(y, y, wide(small[:, 1, :], F), ALU.subtract), base)

            def variance(layer, g, base):
                link(tt(o, y, y, ALU.mult), base)
                link(nc.vector.reduce_sum(small[:, 0, :], o, AX.X), base)
                ts(small[:, 2, :], small[:, 0, :], 1.0 / F, EPS, ALU.mult, ALU.add).then_inc(norm_in, 1)

            def normalise(layer, g, base):
                root, t = small[:, 3, :], small[:, 4, :]
                dve.wait_ge(norm_out, layer * GROUPS + g + 1)
                link(tt(t, root, root, ALU.mult), base)
                link(tt(t, t, small[:, 2, :], ALU.mult), base)
                link(ts(t, t, -0.5, 1.5, ALU.mult, ALU.add), base)
                link(tt(small[:, 5, :], root, t, ALU.mult), base)
                tt(x_sb[:, of_group(g), :], num[:, :, 0:F], wide(small[:, 5, :], F), ALU.mult)\
                    .then_inc(rows_ready, 1)

            for layer in range(2):
                if layer == 1:
                    dve.wait_ge(masks_used, S2_SLOTS + LB)
                    dve.wait_ge(sign_ready, LB)
                prepare(layer)
                multiply(nc.vector, layer, 0)
                take_away(layer, 0, 0)
                if layer == 0:
                    classify(0, 0, 0)
                take_away(layer, 0, 1)
                if layer == 0:
                    compare(0, 0, 0)
                dve.wait_ge(hsum_made, layer + 1)
                nc.vector.tensor_copy(hsum[:, :], acc[:, 1, 0:FE]).then_inc(acc_free, 2)
                for batch in range(BATCHES):
                    q, k = divmod(batch, UNROLL)
                    if batch > 0:
                        classify(layer, 0, batch)
                        compare(layer, 0, batch)
                    if q < QUADS - 1 and 0 < k < PARTS:
                        take_away(layer, q + 1, k - 1)
                    if batch == BATCHES - 4:
                        row_exponents(layer)
                    if batch == BATCHES - 3:
                        clear_u(layer, 1, GROUPS)
                dve.wait_ge(exp_out, 2 * layer + 2)
                pieces = {6: divide, 9: elu, 10: centre, 11: variance, 14: normalise}
                start, steps = count[0], FINISH_STEPS[layer]
                with dve.Fori(1, GROUPS) as g:
                    base = (g - 1) * steps
                    for batch in range(BATCHES):
                        if batch == SUM_AFTER + 1:
                            add_parts(layer, g - 1, halves=(0,))
                        classify(layer, g, batch)
                        if batch == SUM_AFTER + 1:
                            add_parts(layer, g - 1, halves=(1,))
                        compare(layer, g, batch)
                        if batch == min(pieces):
                            dve.wait_ge(combined, layer * (GROUPS - 1) + g)
                        if batch == FLAG_AFTER:
                            dve.wait_ge(stage_read, FREE + layer * GROUPS + g)
                            ts(small[:, 0, :], num[:, :, F], 0.0, None, ALU.is_equal).then_inc(alone_found, 1)
                        if batch in pieces:
                            pieces[batch](layer, g - 1, base)
                assert count[0] - start == steps
                count[0] = start + (GROUPS - 1) * steps
                add_parts(layer, GROUPS - 1)
                if layer == 1:
                    for piece in (scale, mean_if_alone, *pieces.values()):
                        piece(layer, GROUPS - 1, 0)
    return nc


def kernel(x, adj, L0_gnn_a, L1_gnn_W, L1_gnn_a):
    import concourse.bacc as bacc
    from concourse.bass_utils import run_bass_kernel_spmd

    x, adj, a0, w, a1 = (np.asarray(v) for v in (x, adj, L0_gnn_a, L1_gnn_W, L1_gnn_a))
    adj_t = adj.reshape(GROUPS, GN, BATCHES, JB, P).transpose(0, 2, 4, 3, 1)
    arrays = {
        "x_rows": x.reshape(BLOCKS, P, F).transpose(1, 0, 2),
        "x_cols": x.reshape(GROUPS, HALF, 2, P, F).transpose(2, 4, 0, 1, 3).reshape(2 * F, GROUPS, HALF * P),
        "adj_t": adj_t.reshape(GROUPS * BATCHES * P, JB * GN),
        "a0_row": a0.T,
        "a0": a0.reshape(2, F).T,
        "a1": a1.reshape(2, F).T,
        "w": w,
        "w_t": w.T,
    }
    arrays = {name: np.ascontiguousarray(v) for name, v in arrays.items()}
    nc = bacc.Bacc("TRN2", target_bir_lowering=False, num_devices=1)
    args = [nc.dram_tensor(name, v.shape, mybir.dt.from_np(v.dtype), kind="ExternalInput").ap()
            for name, v in arrays.items()]
    out = nc.dram_tensor("out", (P, BLOCKS, F), FP32, kind="ExternalOutput").ap()
    build(nc, *args, out)
    result = run_bass_kernel_spmd(nc, [arrays], core_ids=[0]).results[0]["out"]
    return result.transpose(1, 0, 2).reshape(N, F)
```
